# Optimizing a Trainium2 kernel written in Bass

```python
import numpy as np
import jax
import jax.numpy as jnp

def _softmax(x, axis=-1):
    return jax.nn.softmax(x, axis=axis)

def _gelu(x):
    return jax.nn.gelu(x, approximate=True)

def _silu(x):
    return jax.nn.silu(x)

def _sigmoid(x):
    return jax.nn.sigmoid(x)

def _layernorm(x, axis=-1, eps=1e-05):
    m = jnp.mean(x, axis=axis, keepdims=True)
    v = jnp.var(x, axis=axis, keepdims=True)
    return (x - m) / jnp.sqrt(v + eps)

def _scatter_add(tgt, idx, src, axis=0):
    return tgt.at[idx].add(src)

def _segment_sum(src, seg, n):
    return jax.ops.segment_sum(src, seg, n)
kernel_name = 'mk_pixart_seq_d4_seqx_r8_caa962'

def setup_inputs(seed: int=0):
    np.random.seed(seed)
    _w = jnp.asarray

    def _rec_inputs():
        import jax
        import jax.numpy as jnp
        _rk = jax.random.key(seed)
        x = -0.0005207 + 1.001 * jax.random.normal(jax.random.fold_in(_rk, 1), (4, 512, 128), jnp.float32)
        _lenS = 512 - jax.random.randint(jax.random.fold_in(_rk, 7), (4,), 0, max(1, 512 // 4) + 1, jnp.int32)
        _lenS2 = 77 - jax.random.randint(jax.random.fold_in(_rk, 8), (4,), 0, max(1, 77 // 4) + 1, jnp.int32)
        cond_1024 = 0.000887014 + 1.03683 * jax.random.normal(jax.random.fold_in(_rk, 11), (4, 128), jnp.float32)
        _ctx_768P = jax.random.normal(jax.random.fold_in(_rk, 12), (4, 16, 96), jnp.float32)
        _ctx_768c = jax.random.dirichlet(jax.random.fold_in(_rk, 512), 0.3 * jnp.ones((16,), jnp.float32), (4, 77))
        _ctx_768t = jnp.einsum('bsk,bkd->bsd', _ctx_768c, _ctx_768P)
        _ctx_768t = _ctx_768t * jax.lax.rsqrt(jnp.mean(jnp.square(_ctx_768t)) + 1e-12) * 0.953939
        ctx_768 = 0.000599585 + 1.00006 * (_ctx_768t + 0.3 * jax.random.normal(jax.random.fold_in(_rk, 612), (4, 77, 96), jnp.float32))
        return (x, cond_1024, ctx_768)
    x, cond_1024, ctx_768 = _rec_inputs()

    def _L0_xcond_setup():
        import jax, jax.numpy as jnp
        import numpy as np
        B, N, M = (2, 128, 64)
        D, H, DH = (128, 16, 64)
        MID = H * DH
        DC = 96
        MULT = 4
        EPS = 1e-05

        def _ln(x, w, b):
            mu = jnp.mean(x, -1, keepdims=True)
            var = jnp.mean((x - mu) ** 2, -1, keepdims=True)
            return (x - mu) * jax.lax.rsqrt(var + EPS) * w + b

        def _sincos(n, d):
            inv = 1.0 / 10000.0 ** (jnp.arange(0, d, 2, dtype=jnp.float32) / d)
            ang = jnp.arange(n, dtype=jnp.float32)[:, None] * inv[None, :]
            return (jnp.sin(ang), jnp.cos(ang))

        def _rope(x, sin, cos):
            s = sin[None, None]
            c = cos[None, None]
            xe = x[..., ::2]
            xo = x[..., 1::2]
            re = xe * c - xo * s
            ro = xe * s + xo * c
            return jnp.stack((re, ro), axis=-1).reshape(x.shape)

        def _heads(t):
            b, n, _ = t.shape
            return t.reshape(b, n, H, DH).transpose(0, 2, 1, 3)

        def _attn(xq, ctx, wq, wkv, wo, bo):
            q = _heads(xq @ wq)
            k, v = jnp.split(ctx @ wkv, 2, axis=-1)
            k = _heads(k)
            v = _heads(v)
            sq, cq = _sincos(q.shape[2], DH)
            sk, ck = _sincos(k.shape[2], DH)
            q = _rope(q, sq, cq)
            k = _rope(k, sk, ck)
            sim = jnp.einsum('bhnd,bhmd->bhnm', q, k) * DH ** (-0.5)
            a = jax.nn.softmax(sim, axis=-1)
            o = jnp.einsum('bhnm,bhmd->bhnd', a, v)
            o = o.transpose(0, 2, 1, 3).reshape(xq.shape[0], xq.shape[1], MID)
            return o @ wo + bo

        def _adaln(x, c, lw, lb, gw, gb, bw, bb):
            g = (c @ gw + gb)[:, None, :]
            bt = (c @ bw + bb)[:, None, :]
            return _ln(x, lw, lb) * (1.0 + g) + bt
        ks = jax.random.split(jax.random.key(seed), 24)
        s = 0.02
        inp = {'x': jax.random.normal(ks[0], (B, N, D), jnp.float32), 'cond': jax.random.normal(ks[1], (B, D), jnp.float32), 'context': jax.random.normal(ks[2], (B, M, DC), jnp.float32), 'ln1_w': jnp.ones((D,), jnp.float32), 'ln1_b': jnp.zeros((D,), jnp.float32), 'g1_w': jax.random.normal(ks[3], (D, D), jnp.float32) * s, 'g1_b': jnp.zeros((D,), jnp.float32), 'b1_w': jax.random.normal(ks[4], (D, D), jnp.float32) * s, 'b1_b': jnp.zeros((D,), jnp.float32), 'ln2_w': jnp.ones((D,), jnp.float32), 'ln2_b': jnp.zeros((D,), jnp.float32), 'g2_w': jax.random.normal(ks[5], (D, D), jnp.float32) * s, 'g2_b': jnp.zeros((D,), jnp.float32), 'b2_w': jax.random.normal(ks[6], (D, D), jnp.float32) * s, 'b2_b': jnp.zeros((D,), jnp.float32), 'sa_wq': jax.random.normal(ks[7], (D, MID), jnp.float32) * s, 'sa_wkv': jax.random.normal(ks[8], (D, 2 * MID), jnp.float32) * s, 'sa_wo': jax.random.normal(ks[9], (MID, D), jnp.float32) * s, 'sa_bo': jnp.zeros((D,), jnp.float32), 'ca_lnc_w': jnp.ones((DC,), jnp.float32), 'ca_lnc_b': jnp.zeros((DC,), jnp.float32), 'ca_wq': jax.random.normal(ks[10], (D, MID), jnp.float32) * s, 'ca_wkv': jax.random.normal(ks[11], (DC, 2 * MID), jnp.float32) * s, 'ca_wo': jax.random.normal(ks[12], (MID, D), jnp.float32) * s, 'ca_bo': jnp.zeros((D,), jnp.float32), 'ff_w1': jax.random.normal(ks[13], (D, MULT * D), jnp.float32) * s, 'ff_b1': jnp.zeros((MULT * D,), jnp.float32), 'ff_w2': jax.random.normal(ks[14], (MULT * D, D), jnp.float32) * s, 'ff_b2': jnp.zeros((D,), jnp.float32)}
        return inp
    _L0_xcond_all = _L0_xcond_setup()
    _L0_xcond_in = {k: v for k, v in _L0_xcond_all.items() if k in ('ln1_w', 'ln1_b', 'g1_w', 'g1_b', 'b1_w', 'b1_b', 'ln2_w', 'ln2_b', 'g2_w', 'g2_b', 'b2_w', 'b2_b', 'sa_wq', 'sa_wkv', 'sa_wo', 'sa_bo', 'ca_lnc_w', 'ca_lnc_b', 'ca_wq', 'ca_wkv', 'ca_wo', 'ca_bo', 'ff_w1', 'ff_b1', 'ff_w2', 'ff_b2')}
    del _L0_xcond_all

    def _L1_xcond_setup():
        import jax, jax.numpy as jnp
        import numpy as np
        EPS = 1e-06

        def ln(x, eps=EPS):
            m = jnp.mean(x, axis=-1, keepdims=True)
            v = jnp.mean(jnp.square(x - m), axis=-1, keepdims=True)
            return (x - m) * jax.lax.rsqrt(v + eps)

        def modulate(x, shift, scale):
            return x * (1.0 + scale[:, None, :]) + shift[:, None, :]

        def _heads(t, H):
            B, N, D = t.shape
            return t.reshape(B, N, H, D // H).transpose(0, 2, 1, 3)

        def _unheads(t):
            B, H, N, hd = t.shape
            return t.transpose(0, 2, 1, 3).reshape(B, N, H * hd)
        key = jax.random.key(seed)
        B, N, D, H, T, CD = (4, 128, 128, 16, 32, 96)
        FF = 4 * D
        ks = jax.random.split(key, 20)
        s = 0.02
        return {'x': jax.random.normal(ks[0], (B, N, D), jnp.float32), 'c': jax.random.normal(ks[1], (B, D), jnp.float32), 'brain_tokens': jax.random.normal(ks[2], (B, T, CD), jnp.float32), 'adaln_w': jax.random.normal(ks[3], (9 * D, D), jnp.float32) * s, 'adaln_b': jax.random.normal(ks[4], (9 * D,), jnp.float32) * s, 'qn_w': jnp.ones((D // H,), jnp.float32), 'qn_b': jnp.zeros((D // H,), jnp.float32), 'kn_w': jnp.ones((D // H,), jnp.float32), 'kn_b': jnp.zeros((D // H,), jnp.float32), 'ca_in_w': jax.random.normal(ks[5], (3 * D, D), jnp.float32) * s, 'ca_in_b': jax.random.normal(ks[6], (3 * D,), jnp.float32) * s, 'ca_out_w': jax.random.normal(ks[7], (D, D), jnp.float32) * s, 'ca_out_b': jax.random.normal(ks[8], (D,), jnp.float32) * s, 'cond_w': jax.random.normal(ks[9], (D, CD), jnp.float32) * s, 'cond_b': jax.random.normal(ks[10], (D,), jnp.float32) * s, 'w1': jax.random.normal(ks[11], (FF, D), jnp.float32) * s, 'w3': jax.random.normal(ks[12], (FF, D), jnp.float32) * s, 'w2': jax.random.normal(ks[13], (D, FF), jnp.float32) * s}
    _L1_xcond_all = _L1_xcond_setup()
    _L1_xcond_in = {k: v for k, v in _L1_xcond_all.items() if k in ('adaln_w', 'adaln_b', 'qn_w', 'qn_b', 'kn_w', 'kn_b', 'ca_in_w', 'ca_in_b', 'ca_out_w', 'ca_out_b', 'cond_w', 'cond_b', 'w1', 'w3', 'w2')}
    del _L1_xcond_all

    def _L2_xcond_setup():
        import jax, jax.numpy as jnp
        import numpy as np
        EPS = 1e-05

        def _ada_ln(x, t, W, b):
            emb = t @ W + b
            scale, shift = jnp.split(emb, 2, axis=-1)
            mu = x.mean(-1, keepdims=True)
            var = ((x - mu) ** 2).mean(-1, keepdims=True)
            xn = (x - mu) * jax.lax.rsqrt(var + EPS)
            return xn * (1.0 + scale) + shift

        def _attn(x, ctx, Wq, Wk, Wv, Wo, bo, heads):
            b, n, _ = x.shape
            j = ctx.shape[1]
            q = (x @ Wq).reshape(b, n, heads, -1)
            k = (ctx @ Wk).reshape(b, j, heads, -1)
            v = (ctx @ Wv).reshape(b, j, heads, -1)
            scale = q.shape[-1] ** (-0.5)
            sim = jnp.einsum('bihd,bjhd->bhij', q, k) * scale
            attn = jax.nn.softmax(sim, axis=-1)
            out = jnp.einsum('bhij,bjhd->bihd', attn, v).reshape(b, n, -1)
            return out @ Wo + bo

        def _ff(x, W1, b1, W2, b2):
            p = x @ W1 + b1
            a, gate = jnp.split(p, 2, axis=-1)
            return a * jax.nn.gelu(gate, approximate=False) @ W2 + b2
        key = jax.random.key(seed)
        ks = jax.random.split(key, 32)
        B, N, D = (4, 256, 128)
        J, CD = (32, 96)
        H, DH = (16, 64)
        INNER = H * DH
        FF = 4 * D
        w = lambda k, shp: jax.random.normal(k, shp, jnp.float32) * 0.02
        inp = {'x': jax.random.normal(ks[0], (B, N, D), jnp.float32), 't': jax.random.normal(ks[1], (B, 1, D), jnp.float32), 'context': jax.random.normal(ks[2], (B, J, CD), jnp.float32), 'n1_w': w(ks[3], (D, 2 * D)), 'n1_b': jnp.zeros((2 * D,), jnp.float32), 'n2_w': w(ks[4], (D, 2 * D)), 'n2_b': jnp.zeros((2 * D,), jnp.float32), 'n3_w': w(ks[5], (D, 2 * D)), 'n3_b': jnp.zeros((2 * D,), jnp.float32), 'q1': w(ks[6], (D, INNER)), 'k1': w(ks[7], (D, INNER)), 'v1': w(ks[8], (D, INNER)), 'o1_w': w(ks[9], (INNER, D)), 'o1_b': jnp.zeros((D,), jnp.float32), 'q2': w(ks[10], (D, INNER)), 'k2': w(ks[11], (CD, INNER)), 'v2': w(ks[12], (CD, INNER)), 'o2_w': w(ks[13], (INNER, D)), 'o2_b': jnp.zeros((D,), jnp.float32), 'ff_w1': w(ks[14], (D, 2 * FF)), 'ff_b1': jnp.zeros((2 * FF,), jnp.float32), 'ff_w2': w(ks[15], (FF, D)), 'ff_b2': jnp.zeros((D,), jnp.float32)}
        return inp
    _L2_xcond_all = _L2_xcond_setup()
    _L2_xcond_in = {k: v for k, v in _L2_xcond_all.items() if k in ('n1_w', 'n1_b', 'n2_w', 'n2_b', 'n3_w', 'n3_b', 'q1', 'k1', 'v1', 'o1_w', 'o1_b', 'q2', 'k2', 'v2', 'o2_w', 'o2_b', 'ff_w1', 'ff_b1', 'ff_w2', 'ff_b2')}
    del _L2_xcond_all

    def _L3_xcond_setup():
        import jax, jax.numpy as jnp
        import numpy as np
        B, N, D, H, TD, TL = (4, 128, 128, 16, 96, 77)
        HD = D // H
        EPS = 1e-06

        def _ln(x):
            mu = jnp.mean(x, axis=-1, keepdims=True)
            var = jnp.var(x, axis=-1, keepdims=True)
            return (x - mu) * jax.lax.rsqrt(var + EPS)

        def _modulate(x, shift, scale):
            return x * (1.0 + scale[:, None, :]) + shift[:, None, :]

        def _heads(t):
            return t.reshape(t.shape[0], t.shape[1], H, HD).transpose(0, 2, 1, 3)

        def _attend(q, k, v):
            sim = jnp.einsum('bhid,bhjd->bhij', q, k) * HD ** (-0.5)
            attn = jax.nn.softmax(sim, axis=-1)
            out = jnp.einsum('bhij,bhjd->bhid', attn, v)
            return out.transpose(0, 2, 1, 3).reshape(out.shape[0], -1, D)
        key = jax.random.key(seed)
        ks = jax.random.split(key, 16)
        s = 0.02
        return {'x': jax.random.normal(ks[0], (B, N, D), jnp.float32), 'c': jax.random.normal(ks[1], (B, D), jnp.float32), 'text_embed': jax.random.normal(ks[2], (B, TL, TD), jnp.float32), 'W_ada': jax.random.normal(ks[3], (D, 6 * D), jnp.float32) * s, 'b_ada': jnp.zeros((6 * D,), jnp.float32), 'W_qkv': jax.random.normal(ks[4], (D, 3 * D), jnp.float32) * s, 'b_qkv': jnp.zeros((3 * D,), jnp.float32), 'W_proj': jax.random.normal(ks[5], (D, D), jnp.float32) * s, 'b_proj': jnp.zeros((D,), jnp.float32), 'W_ctx': jax.random.normal(ks[6], (TD, D), jnp.float32) * s, 'b_ctx': jnp.zeros((D,), jnp.float32), 'W_q': jax.random.normal(ks[7], (D, D), jnp.float32) * s, 'W_k': jax.random.normal(ks[8], (D, D), jnp.float32) * s, 'W_v': jax.random.normal(ks[9], (D, D), jnp.float32) * s, 'W_out': jax.random.normal(ks[10], (D, D), jnp.float32) * s, 'b_out': jnp.zeros((D,), jnp.float32), 'W_fc1': jax.random.normal(ks[11], (D, 4 * D), jnp.float32) * s, 'b_fc1': jnp.zeros((4 * D,), jnp.float32), 'W_fc2': jax.random.normal(ks[12], (4 * D, D), jnp.float32) * s, 'b_fc2': jnp.zeros((D,), jnp.float32)}
    _L3_xcond_all = _L3_xcond_setup()
    _L3_xcond_in = {k: v for k, v in _L3_xcond_all.items() if k in ('W_ada', 'b_ada', 'W_qkv', 'b_qkv', 'W_proj', 'b_proj', 'W_ctx', 'b_ctx', 'W_q', 'W_k', 'W_v', 'W_out', 'b_out', 'W_fc1', 'b_fc1', 'W_fc2', 'b_fc2')}
    del _L3_xcond_all
    return {'x': x, 'cond_1024': cond_1024, 'ctx_768': ctx_768, 'L0_xcond_ln1_w': _L0_xcond_in['ln1_w'], 'L0_xcond_ln1_b': _L0_xcond_in['ln1_b'], 'L0_xcond_g1_w': _L0_xcond_in['g1_w'], 'L0_xcond_g1_b': _L0_xcond_in['g1_b'], 'L0_xcond_b1_w': _L0_xcond_in['b1_w'], 'L0_xcond_b1_b': _L0_xcond_in['b1_b'], 'L0_xcond_ln2_w': _L0_xcond_in['ln2_w'], 'L0_xcond_ln2_b': _L0_xcond_in['ln2_b'], 'L0_xcond_g2_w': _L0_xcond_in['g2_w'], 'L0_xcond_g2_b': _L0_xcond_in['g2_b'], 'L0_xcond_b2_w': _L0_xcond_in['b2_w'], 'L0_xcond_b2_b': _L0_xcond_in['b2_b'], 'L0_xcond_sa_wq': _L0_xcond_in['sa_wq'], 'L0_xcond_sa_wkv': _L0_xcond_in['sa_wkv'], 'L0_xcond_sa_wo': _L0_xcond_in['sa_wo'], 'L0_xcond_sa_bo': _L0_xcond_in['sa_bo'], 'L0_xcond_ca_lnc_w': _L0_xcond_in['ca_lnc_w'], 'L0_xcond_ca_lnc_b': _L0_xcond_in['ca_lnc_b'], 'L0_xcond_ca_wq': _L0_xcond_in['ca_wq'], 'L0_xcond_ca_wkv': _L0_xcond_in['ca_wkv'], 'L0_xcond_ca_wo': _L0_xcond_in['ca_wo'], 'L0_xcond_ca_bo': _L0_xcond_in['ca_bo'], 'L0_xcond_ff_w1': _L0_xcond_in['ff_w1'], 'L0_xcond_ff_b1': _L0_xcond_in['ff_b1'], 'L0_xcond_ff_w2': _L0_xcond_in['ff_w2'], 'L0_xcond_ff_b2': _L0_xcond_in['ff_b2'], 'L1_xcond_adaln_w': _L1_xcond_in['adaln_w'], 'L1_xcond_adaln_b': _L1_xcond_in['adaln_b'], 'L1_xcond_qn_w': _L1_xcond_in['qn_w'], 'L1_xcond_qn_b': _L1_xcond_in['qn_b'], 'L1_xcond_kn_w': _L1_xcond_in['kn_w'], 'L1_xcond_kn_b': _L1_xcond_in['kn_b'], 'L1_xcond_ca_in_w': _L1_xcond_in['ca_in_w'], 'L1_xcond_ca_in_b': _L1_xcond_in['ca_in_b'], 'L1_xcond_ca_out_w': _L1_xcond_in['ca_out_w'], 'L1_xcond_ca_out_b': _L1_xcond_in['ca_out_b'], 'L1_xcond_cond_w': _L1_xcond_in['cond_w'], 'L1_xcond_cond_b': _L1_xcond_in['cond_b'], 'L1_xcond_w1': _L1_xcond_in['w1'], 'L1_xcond_w3': _L1_xcond_in['w3'], 'L1_xcond_w2': _L1_xcond_in['w2'], 'L2_xcond_n1_w': _L2_xcond_in['n1_w'], 'L2_xcond_n1_b': _L2_xcond_in['n1_b'], 'L2_xcond_n2_w': _L2_xcond_in['n2_w'], 'L2_xcond_n2_b': _L2_xcond_in['n2_b'], 'L2_xcond_n3_w': _L2_xcond_in['n3_w'], 'L2_xcond_n3_b': _L2_xcond_in['n3_b'], 'L2_xcond_q1': _L2_xcond_in['q1'], 'L2_xcond_k1': _L2_xcond_in['k1'], 'L2_xcond_v1': _L2_xcond_in['v1'], 'L2_xcond_o1_w': _L2_xcond_in['o1_w'], 'L2_xcond_o1_b': _L2_xcond_in['o1_b'], 'L2_xcond_q2': _L2_xcond_in['q2'], 'L2_xcond_k2': _L2_xcond_in['k2'], 'L2_xcond_v2': _L2_xcond_in['v2'], 'L2_xcond_o2_w': _L2_xcond_in['o2_w'], 'L2_xcond_o2_b': _L2_xcond_in['o2_b'], 'L2_xcond_ff_w1': _L2_xcond_in['ff_w1'], 'L2_xcond_ff_b1': _L2_xcond_in['ff_b1'], 'L2_xcond_ff_w2': _L2_xcond_in['ff_w2'], 'L2_xcond_ff_b2': _L2_xcond_in['ff_b2'], 'L3_xcond_W_ada': _L3_xcond_in['W_ada'], 'L3_xcond_b_ada': _L3_xcond_in['b_ada'], 'L3_xcond_W_qkv': _L3_xcond_in['W_qkv'], 'L3_xcond_b_qkv': _L3_xcond_in['b_qkv'], 'L3_xcond_W_proj': _L3_xcond_in['W_proj'], 'L3_xcond_b_proj': _L3_xcond_in['b_proj'], 'L3_xcond_W_ctx': _L3_xcond_in['W_ctx'], 'L3_xcond_b_ctx': _L3_xcond_in['b_ctx'], 'L3_xcond_W_q': _L3_xcond_in['W_q'], 'L3_xcond_W_k': _L3_xcond_in['W_k'], 'L3_xcond_W_v': _L3_xcond_in['W_v'], 'L3_xcond_W_out': _L3_xcond_in['W_out'], 'L3_xcond_b_out': _L3_xcond_in['b_out'], 'L3_xcond_W_fc1': _L3_xcond_in['W_fc1'], 'L3_xcond_b_fc1': _L3_xcond_in['b_fc1'], 'L3_xcond_W_fc2': _L3_xcond_in['W_fc2'], 'L3_xcond_b_fc2': _L3_xcond_in['b_fc2']}

def reference(x, cond_1024, ctx_768, L0_xcond_ln1_w, L0_xcond_ln1_b, L0_xcond_g1_w, L0_xcond_g1_b, L0_xcond_b1_w, L0_xcond_b1_b, L0_xcond_ln2_w, L0_xcond_ln2_b, L0_xcond_g2_w, L0_xcond_g2_b, L0_xcond_b2_w, L0_xcond_b2_b, L0_xcond_sa_wq, L0_xcond_sa_wkv, L0_xcond_sa_wo, L0_xcond_sa_bo, L0_xcond_ca_lnc_w, L0_xcond_ca_lnc_b, L0_xcond_ca_wq, L0_xcond_ca_wkv, L0_xcond_ca_wo, L0_xcond_ca_bo, L0_xcond_ff_w1, L0_xcond_ff_b1, L0_xcond_ff_w2, L0_xcond_ff_b2, L1_xcond_adaln_w, L1_xcond_adaln_b, L1_xcond_qn_w, L1_xcond_qn_b, L1_xcond_kn_w, L1_xcond_kn_b, L1_xcond_ca_in_w, L1_xcond_ca_in_b, L1_xcond_ca_out_w, L1_xcond_ca_out_b, L1_xcond_cond_w, L1_xcond_cond_b, L1_xcond_w1, L1_xcond_w3, L1_xcond_w2, L2_xcond_n1_w, L2_xcond_n1_b, L2_xcond_n2_w, L2_xcond_n2_b, L2_xcond_n3_w, L2_xcond_n3_b, L2_xcond_q1, L2_xcond_k1, L2_xcond_v1, L2_xcond_o1_w, L2_xcond_o1_b, L2_xcond_q2, L2_xcond_k2, L2_xcond_v2, L2_xcond_o2_w, L2_xcond_o2_b, L2_xcond_ff_w1, L2_xcond_ff_b1, L2_xcond_ff_w2, L2_xcond_ff_b2, L3_xcond_W_ada, L3_xcond_b_ada, L3_xcond_W_qkv, L3_xcond_b_qkv, L3_xcond_W_proj, L3_xcond_b_proj, L3_xcond_W_ctx, L3_xcond_b_ctx, L3_xcond_W_q, L3_xcond_W_k, L3_xcond_W_v, L3_xcond_W_out, L3_xcond_b_out, L3_xcond_W_fc1, L3_xcond_b_fc1, L3_xcond_W_fc2, L3_xcond_b_fc2):
    import jax
    import jax.numpy as jnp

    def _L0_xcond_ref(x, cond, context, ln1_w, ln1_b, g1_w, g1_b, b1_w, b1_b, ln2_w, ln2_b, g2_w, g2_b, b2_w, b2_b, sa_wq, sa_wkv, sa_wo, sa_bo, ca_lnc_w, ca_lnc_b, ca_wq, ca_wkv, ca_wo, ca_bo, ff_w1, ff_b1, ff_w2, ff_b2):
        import jax, jax.numpy as jnp
        import numpy as np
        B, N, M = (2, 128, 64)
        D, H, DH = (128, 16, 64)
        MID = H * DH
        DC = 96
        MULT = 4
        EPS = 1e-05

        def _ln(x, w, b):
            mu = jnp.mean(x, -1, keepdims=True)
            var = jnp.mean((x - mu) ** 2, -1, keepdims=True)
            return (x - mu) * jax.lax.rsqrt(var + EPS) * w + b

        def _sincos(n, d):
            inv = 1.0 / 10000.0 ** (jnp.arange(0, d, 2, dtype=jnp.float32) / d)
            ang = jnp.arange(n, dtype=jnp.float32)[:, None] * inv[None, :]
            return (jnp.sin(ang), jnp.cos(ang))

        def _rope(x, sin, cos):
            s = sin[None, None]
            c = cos[None, None]
            xe = x[..., ::2]
            xo = x[..., 1::2]
            re = xe * c - xo * s
            ro = xe * s + xo * c
            return jnp.stack((re, ro), axis=-1).reshape(x.shape)

        def _heads(t):
            b, n, _ = t.shape
            return t.reshape(b, n, H, DH).transpose(0, 2, 1, 3)

        def _attn(xq, ctx, wq, wkv, wo, bo):
            q = _heads(xq @ wq)
            k, v = jnp.split(ctx @ wkv, 2, axis=-1)
            k = _heads(k)
            v = _heads(v)
            sq, cq = _sincos(q.shape[2], DH)
            sk, ck = _sincos(k.shape[2], DH)
            q = _rope(q, sq, cq)
            k = _rope(k, sk, ck)
            sim = jnp.einsum('bhnd,bhmd->bhnm', q, k) * DH ** (-0.5)
            a = jax.nn.softmax(sim, axis=-1)
            o = jnp.einsum('bhnm,bhmd->bhnd', a, v)
            o = o.transpose(0, 2, 1, 3).reshape(xq.shape[0], xq.shape[1], MID)
            return o @ wo + bo

        def _adaln(x, c, lw, lb, gw, gb, bw, bb):
            g = (c @ gw + gb)[:, None, :]
            bt = (c @ bw + bb)[:, None, :]
            return _ln(x, lw, lb) * (1.0 + g) + bt
        attn_in = _adaln(x, cond, ln1_w, ln1_b, g1_w, g1_b, b1_w, b1_b)
        x = _attn(attn_in, attn_in, sa_wq, sa_wkv, sa_wo, sa_bo) + x
        cross_in = _adaln(x, cond, ln1_w, ln1_b, g1_w, g1_b, b1_w, b1_b)
        ctx_n = _ln(context, ca_lnc_w, ca_lnc_b)
        x = _attn(cross_in, ctx_n, ca_wq, ca_wkv, ca_wo, ca_bo) + x
        ffn_in = _adaln(x, cond, ln2_w, ln2_b, g2_w, g2_b, b2_w, b2_b)
        h = jax.nn.gelu(ffn_in @ ff_w1 + ff_b1, approximate=False)
        x = h @ ff_w2 + ff_b2 + x
        return x

    def _L1_xcond_ref(x, c, brain_tokens, adaln_w, adaln_b, qn_w, qn_b, kn_w, kn_b, ca_in_w, ca_in_b, ca_out_w, ca_out_b, cond_w, cond_b, w1, w3, w2):
        import jax, jax.numpy as jnp
        import numpy as np
        EPS = 1e-06

        def ln(x, eps=EPS):
            m = jnp.mean(x, axis=-1, keepdims=True)
            v = jnp.mean(jnp.square(x - m), axis=-1, keepdims=True)
            return (x - m) * jax.lax.rsqrt(v + eps)

        def modulate(x, shift, scale):
            return x * (1.0 + scale[:, None, :]) + shift[:, None, :]

        def _heads(t, H):
            B, N, D = t.shape
            return t.reshape(B, N, H, D // H).transpose(0, 2, 1, 3)

        def _unheads(t):
            B, H, N, hd = t.shape
            return t.transpose(0, 2, 1, 3).reshape(B, N, H * hd)
        B, N, D = x.shape
        H = 16
        hd = D // H
        scale = hd ** (-0.5)
        mod = jax.nn.silu(c) @ adaln_w.T + adaln_b
        shift_sa, scale_sa, gate_sa, shift_ca, scale_ca, gate_ca, shift_ff, scale_ff, gate_ff = jnp.split(mod, 9, axis=-1)
        h = modulate(ln(x), shift_sa, scale_sa)
        q = ln(_heads(h, H)) * qn_w + qn_b
        k = ln(_heads(h, H)) * kn_w + kn_b
        v = _heads(h, H)
        attn = jax.nn.softmax(jnp.einsum('bhqd,bhkd->bhqk', q, k) * scale, axis=-1)
        h = _unheads(jnp.einsum('bhqk,bhkd->bhqd', attn, v))
        x = x + gate_sa[:, None, :] * h
        h = modulate(ln(x), shift_ca, scale_ca)
        kv = brain_tokens @ cond_w.T + cond_b
        wq, wk, wv = jnp.split(ca_in_w, 3, axis=0)
        bq, bk, bv = jnp.split(ca_in_b, 3, axis=0)
        q = _heads(h @ wq.T + bq, H)
        k = _heads(kv @ wk.T + bk, H)
        v = _heads(kv @ wv.T + bv, H)
        attn = jax.nn.softmax(jnp.einsum('bhqd,bhkd->bhqk', q, k) * scale, axis=-1)
        h = _unheads(jnp.einsum('bhqk,bhkd->bhqd', attn, v)) @ ca_out_w.T + ca_out_b
        x = x + gate_ca[:, None, :] * h
        h = modulate(ln(x), shift_ff, scale_ff)
        h = jax.nn.silu(h @ w1.T) * (h @ w3.T) @ w2.T
        x = x + gate_ff[:, None, :] * h
        return x

    def _L2_xcond_ref(x, t, context, n1_w, n1_b, n2_w, n2_b, n3_w, n3_b, q1, k1, v1, o1_w, o1_b, q2, k2, v2, o2_w, o2_b, ff_w1, ff_b1, ff_w2, ff_b2):
        import jax, jax.numpy as jnp
        import numpy as np
        EPS = 1e-05

        def _ada_ln(x, t, W, b):
            emb = t @ W + b
            scale, shift = jnp.split(emb, 2, axis=-1)
            mu = x.mean(-1, keepdims=True)
            var = ((x - mu) ** 2).mean(-1, keepdims=True)
            xn = (x - mu) * jax.lax.rsqrt(var + EPS)
            return xn * (1.0 + scale) + shift

        def _attn(x, ctx, Wq, Wk, Wv, Wo, bo, heads):
            b, n, _ = x.shape
            j = ctx.shape[1]
            q = (x @ Wq).reshape(b, n, heads, -1)
            k = (ctx @ Wk).reshape(b, j, heads, -1)
            v = (ctx @ Wv).reshape(b, j, heads, -1)
            scale = q.shape[-1] ** (-0.5)
            sim = jnp.einsum('bihd,bjhd->bhij', q, k) * scale
            attn = jax.nn.softmax(sim, axis=-1)
            out = jnp.einsum('bhij,bjhd->bihd', attn, v).reshape(b, n, -1)
            return out @ Wo + bo

        def _ff(x, W1, b1, W2, b2):
            p = x @ W1 + b1
            a, gate = jnp.split(p, 2, axis=-1)
            return a * jax.nn.gelu(gate, approximate=False) @ W2 + b2
        H = 16
        h = _ada_ln(x, t, n1_w, n1_b)
        x = _attn(h, h, q1, k1, v1, o1_w, o1_b, H) + x
        h = _ada_ln(x, t, n2_w, n2_b)
        x = _attn(h, context, q2, k2, v2, o2_w, o2_b, H) + x
        h = _ada_ln(x, t, n3_w, n3_b)
        x = _ff(h, ff_w1, ff_b1, ff_w2, ff_b2) + x
        return x

    def _L3_xcond_ref(x, c, text_embed, W_ada, b_ada, W_qkv, b_qkv, W_proj, b_proj, W_ctx, b_ctx, W_q, W_k, W_v, W_out, b_out, W_fc1, b_fc1, W_fc2, b_fc2):
        import jax, jax.numpy as jnp
        import numpy as np
        B, N, D, H, TD, TL = (4, 128, 128, 16, 96, 77)
        HD = D // H
        EPS = 1e-06

        def _ln(x):
            mu = jnp.mean(x, axis=-1, keepdims=True)
            var = jnp.var(x, axis=-1, keepdims=True)
            return (x - mu) * jax.lax.rsqrt(var + EPS)

        def _modulate(x, shift, scale):
            return x * (1.0 + scale[:, None, :]) + shift[:, None, :]

        def _heads(t):
            return t.reshape(t.shape[0], t.shape[1], H, HD).transpose(0, 2, 1, 3)

        def _attend(q, k, v):
            sim = jnp.einsum('bhid,bhjd->bhij', q, k) * HD ** (-0.5)
            attn = jax.nn.softmax(sim, axis=-1)
            out = jnp.einsum('bhij,bhjd->bhid', attn, v)
            return out.transpose(0, 2, 1, 3).reshape(out.shape[0], -1, D)
        mod = jax.nn.silu(c) @ W_ada + b_ada
        sh_msa, sc_msa, sh_x, sc_x, sh_mlp, sc_mlp = jnp.split(mod, 6, axis=-1)
        h1 = _modulate(_ln(x), sh_msa, sc_msa)
        qkv = h1 @ W_qkv + b_qkv
        q, k, v = jnp.split(qkv, 3, axis=-1)
        out = _attend(_heads(q), _heads(k), _heads(v))
        x = x + (out @ W_proj + b_proj)
        h2 = _modulate(_ln(x), sh_x, sc_x)
        ctx = text_embed @ W_ctx + b_ctx
        q = _heads(h2 @ W_q)
        k = _heads(ctx @ W_k)
        v = _heads(ctx @ W_v)
        out = _attend(q, k, v)
        x = x + (out @ W_out + b_out)
        h3 = _modulate(_ln(x), sh_mlp, sc_mlp)
        hidden = jax.nn.gelu(h3 @ W_fc1 + b_fc1, approximate=True)
        x = x + (hidden @ W_fc2 + b_fc2)
        return x
    x = _L0_xcond_ref(x, cond_1024, ctx_768, L0_xcond_ln1_w, L0_xcond_ln1_b, L0_xcond_g1_w, L0_xcond_g1_b, L0_xcond_b1_w, L0_xcond_b1_b, L0_xcond_ln2_w, L0_xcond_ln2_b, L0_xcond_g2_w, L0_xcond_g2_b, L0_xcond_b2_w, L0_xcond_b2_b, L0_xcond_sa_wq, L0_xcond_sa_wkv, L0_xcond_sa_wo, L0_xcond_sa_bo, L0_xcond_ca_lnc_w, L0_xcond_ca_lnc_b, L0_xcond_ca_wq, L0_xcond_ca_wkv, L0_xcond_ca_wo, L0_xcond_ca_bo, L0_xcond_ff_w1, L0_xcond_ff_b1, L0_xcond_ff_w2, L0_xcond_ff_b2)
    x = _L1_xcond_ref(x, cond_1024, ctx_768, L1_xcond_adaln_w, L1_xcond_adaln_b, L1_xcond_qn_w, L1_xcond_qn_b, L1_xcond_kn_w, L1_xcond_kn_b, L1_xcond_ca_in_w, L1_xcond_ca_in_b, L1_xcond_ca_out_w, L1_xcond_ca_out_b, L1_xcond_cond_w, L1_xcond_cond_b, L1_xcond_w1, L1_xcond_w3, L1_xcond_w2)
    x = _L2_xcond_ref(x, cond_1024[:, None, :], ctx_768, L2_xcond_n1_w, L2_xcond_n1_b, L2_xcond_n2_w, L2_xcond_n2_b, L2_xcond_n3_w, L2_xcond_n3_b, L2_xcond_q1, L2_xcond_k1, L2_xcond_v1, L2_xcond_o1_w, L2_xcond_o1_b, L2_xcond_q2, L2_xcond_k2, L2_xcond_v2, L2_xcond_o2_w, L2_xcond_o2_b, L2_xcond_ff_w1, L2_xcond_ff_b1, L2_xcond_ff_w2, L2_xcond_ff_b2)
    x = _L3_xcond_ref(x, cond_1024, ctx_768, L3_xcond_W_ada, L3_xcond_b_ada, L3_xcond_W_qkv, L3_xcond_b_qkv, L3_xcond_W_proj, L3_xcond_b_proj, L3_xcond_W_ctx, L3_xcond_b_ctx, L3_xcond_W_q, L3_xcond_W_k, L3_xcond_W_v, L3_xcond_W_out, L3_xcond_b_out, L3_xcond_W_fc1, L3_xcond_b_fc1, L3_xcond_W_fc2, L3_xcond_b_fc2)
    return x

_drawn_inputs = setup_inputs


def setup_inputs(seed=0):
    import zlib

    import numpy as np

    out = dict(_drawn_inputs(seed))
    spreads = {'L0_xcond_ln1_w': (1.0, 0.6),
     'L0_xcond_ln1_b': (0.0, 0.573),
     'L0_xcond_g1_b': (0.0, 0.8),
     'L0_xcond_b1_b': (0.0, 0.527),
     'L0_xcond_ln2_w': (1.0, 0.6),
     'L0_xcond_ln2_b': (0.0, 0.8),
     'L0_xcond_g2_b': (0.0, 0.8),
     'L0_xcond_b2_b': (0.0, 0.8),
     'L0_xcond_sa_bo': (0.0, 0.1),
     'L0_xcond_ca_lnc_w': (1.0, 0.6),
     'L0_xcond_ca_lnc_b': (0.0, 0.649),
     'L0_xcond_ca_bo': (0.0, 0.1),
     'L0_xcond_ff_b1': (0.0, 0.357),
     'L0_xcond_ff_b2': (0.0, 0.1),
     'L1_xcond_qn_w': (1.0, 0.6),
     'L1_xcond_qn_b': (0.0, 0.8),
     'L1_xcond_kn_w': (1.0, 0.6),
     'L1_xcond_kn_b': (0.0, 2.0),
     'L2_xcond_n1_b': (0.0, 0.615),
     'L2_xcond_n2_b': (0.0, 0.8),
     'L2_xcond_n3_b': (0.0, 0.8),
     'L2_xcond_o1_b': (0.0, 0.1),
     'L2_xcond_o2_b': (0.0, 0.1),
     'L2_xcond_ff_b1': (0.0, 0.8),
     'L2_xcond_ff_b2': (0.0, 0.624),
     'L3_xcond_b_ada': (0.0, 0.8),
     'L3_xcond_b_qkv': (0.0, 2.0),
     'L3_xcond_b_proj': (0.0, 0.558),
     'L3_xcond_b_ctx': (0.0, 0.8),
     'L3_xcond_b_out': (0.0, 0.8),
     'L3_xcond_b_fc1': (0.0, 2.0),
     'L3_xcond_b_fc2': (0.0, 0.8)}
    factors = {'L0_xcond_g1_w': 8.0,
     'L0_xcond_g2_w': 4.333,
     'L0_xcond_b2_w': 4.701,
     'L0_xcond_sa_wq': 8.0,
     'L0_xcond_ca_wq': 8.0,
     'L1_xcond_adaln_b': 5.907,
     'L1_xcond_ca_in_w': 8.0,
     'L1_xcond_ca_in_b': 8.0,
     'L1_xcond_ca_out_w': 8.0,
     'L1_xcond_ca_out_b': 8.0,
     'L1_xcond_cond_w': 8.0,
     'L1_xcond_cond_b': 8.0,
     'L1_xcond_w1': 8.0,
     'L1_xcond_w3': 8.0,
     'L1_xcond_w2': 8.0,
     'L2_xcond_n2_w': 8.0,
     'L2_xcond_n3_w': 8.0,
     'L2_xcond_q1': 8.0,
     'L2_xcond_k1': 8.0,
     'L2_xcond_q2': 8.0,
     'L2_xcond_k2': 8.0,
     'L2_xcond_ff_w1': 3.663,
     'L2_xcond_ff_w2': 3.644,
     'L3_xcond_W_ada': 4.078,
     'L3_xcond_W_qkv': 3.808,
     'L3_xcond_W_ctx': 8.0,
     'L3_xcond_W_q': 8.0,
     'L3_xcond_W_k': 8.0,
     'L3_xcond_W_v': 8.0,
     'L3_xcond_W_out': 8.0,
     'L3_xcond_W_fc1': 5.783,
     'L3_xcond_W_fc2': 4.348}
    for name, (base, spread) in spreads.items():
        noise = np.random.default_rng([zlib.crc32(name.encode()), seed]).standard_normal(out[name].shape)
        drawn = base * np.exp(spread * noise) if base else spread * noise
        out[name] = jnp.asarray(drawn.astype(out[name].dtype))
    for name, factor in factors.items():
        out[name] = (out[name] * factor).astype(out[name].dtype)
    return out
```

```python
from contextlib import ExitStack

import concourse.bass as bass
import concourse.mybir as mybir
import numpy as np

F32 = mybir.dt.float32
BF16 = mybir.dt.bfloat16
ACT = mybir.ActivationFunctionType
ALU = mybir.AluOpType
AXIS_X = mybir.AxisListType.X

P = 128
B, N, D = 4, 512, 128
NC, DC = 77, 96
H = 16
QT = N // P
FF = 4 * D
FC = FF // P
SLOTS = 2
EXP_LN_SET = 6

MOD_SCALES = ["L0g1", "L0g2", "L1sc_sa", "L1sc_ca", "L1sc_ff", "L2s1", "L2s2", "L2s3",
              "L3sc_msa", "L3sc_x", "L3sc_mlp"]
MOD_REST = ["L0b1", "L0b2", "L1sh_sa", "L1sh_ca", "L1sh_ff", "L2t1", "L2t2", "L2t3",
            "L3sh_msa", "L3sh_x", "L3sh_mlp", "L1ga_sa", "L1ga_ca", "L1ga_ff"]
MOD_DERIVED = ["L0A1", "L0B1", "L0A2", "L0B2", "L1gb_ca"]
MODS = MOD_SCALES + MOD_REST + MOD_DERIVED
NM = len(MOD_SCALES) + len(MOD_REST)
MOD = {n: i for i, n in enumerate(MODS)}
LN_MODS = {(0, 0): ("L0A1", "L0B1"), (0, 1): ("L0A1", "L0B1"), (0, 2): ("L0A2", "L0B2"),
           (1, 0): ("L1sc_sa", "L1sh_sa"), (1, 1): ("L1sc_ca", "L1sh_ca"), (1, 2): ("L1sc_ff", "L1sh_ff"),
           (2, 0): ("L2s1", "L2t1"), (2, 1): ("L2s2", "L2t2"), (2, 2): ("L2s3", "L2t3"),
           (3, 0): ("L3sc_msa", "L3sh_msa"), (3, 1): ("L3sc_x", "L3sh_x"), (3, 2): ("L3sc_mlp", "L3sh_mlp")}
LN_EPS = ["eps5", "eps6", "eps5", "eps6"]

VECS = (["eps5", "eps6", "lw1", "lb1", "lw2", "lb2", "cw", "cb", "L1cond_b", "L3b_ctx", "L1bo_ca",
         "L0bo_sa", "L0bo_ca", "L0ff_b2", "L2bo_sa", "L2bo_ca", "L2ff_b2", "L3bo_sa", "L3bo_ca", "L3ff_b2",
         "qn_w", "qn_b", "kn_w", "kn_b", "qmask", "kmask", "kones"]
        + [f"L0ff_b1_{c}" for c in range(FC)] + [f"L3ff_b1_{c}" for c in range(FC)]
        + [f"L2ff_a_{c}" for c in range(FC)] + [f"L2ff_g_{c}" for c in range(FC)]
        + [f"{a}_b{w}{m}_{g}" for a in ("L1c", "L3s") for w in "qk" for m in ("", "m") for g in range(4)])
VEC = {n: i for i, n in enumerate(VECS)}

KEPT = [("avg", P), ("avg8", P), ("dsel", P), ("ones", 64), ("rope_c", N), ("rope_s", N),
        ("L0ff1", FF), ("L0ff2", FF),
        ("pick_qk", 512), ("pick_v", 512), ("L1s_wo", 512), ("L1c_q", 512), ("L1c_k", 512), ("L1c_v", 512),
        ("L1c_wo", 512), ("L1w1", FF), ("L1w3", FF), ("L1w2", FF), ("L1c_bv", 512),
        ("L2ff1", 2 * FF), ("L2ff2", FF),
        ("L3s_q", 512), ("L3s_k", 512), ("L3s_v", 512), ("L3s_wo", 512), ("L3s_bv", 512),
        ("L3c_q", 512), ("L3c_k", 512), ("L3c_v", 512), ("L3c_wo", 512), ("L3ff1", FF), ("L3ff2", FF),
        ("bv_ones", 512)]
WIDE0 = [("q", 1024), ("k", 1024), ("v", 1024), ("wo", 1024), ("qs", 1024), ("ks", 1024)]


def offsets(pieces):
    at, out = 0, {}
    for name, n in pieces:
        out[name] = (at, n)
        at += n
    return out, at


KEPT_AT, KEPT_N = offsets(KEPT)
WIDE_AT, WIDE_N = offsets(WIDE0)
WIDE2_N = 4 * 1024


class Attention:

    def __init__(self, layer, cross):
        self.layer, self.cross = layer, cross
        self.wide = layer in (0, 2)
        self.dh = 64 if self.wide else 8
        self.rope = layer == 0
        self.heads = 2 if self.wide else 4
        self.groups = H // self.heads
        self.block = P // self.heads
        self.keys = NC if cross else N
        self.tiles = [NC] if cross else [P] * QT
        self.lead = 2 if self.wide else 5
        self.scale = float(self.dh) ** -0.5
        self.name = f"L{layer}{'c' if cross else 's'}"
        self.vcols = H * (64 if self.wide else 32)


ATTENTIONS = [Attention(layer, cross) for layer in range(4) for cross in (False, True)]


class Step:

    def __init__(self, kind, a=None, s=None, g=None, u=None, t=None, c=None, ln=None, head_norm=False, layer=None):
        self.kind, self.a, self.s, self.layer = kind, a, s, layer
        self.g, self.u, self.t, self.c = g, u, t, c
        self.ln, self.head_norm = ln, head_norm


def dense_before(a, s):
    steps = [Step("mean", s=s, ln=(a.layer, int(a.cross)), head_norm=False),
             Step("var", s=s, ln=(a.layer, int(a.cross)), head_norm=False)]
    if a.layer == 1 and not a.cross:
        steps += [Step("mean", s=s, ln=(1, "qk"), head_norm=True), Step("var", s=s, ln=(1, "qk"), head_norm=True)]
    steps += [Step("v", s=s, a=a, t=t, c=c) for t in range(len(a.tiles)) for c in range(a.vcols // 512)]
    return steps


def feed_forward(layer, s):
    steps = [Step("mean", s=s, ln=(layer, 2), head_norm=False), Step("var", s=s, ln=(layer, 2), head_norm=False)]
    steps += [Step("up", s=s, layer=layer, c=c) for c in range(FC)]
    return steps + [Step("down", s=s, layer=layer)]


def attention_steps(a, fill0, fill1):
    out = []
    nh, ng, nt = SLOTS * H, SLOTS * a.groups, len(a.tiles)
    late = []

    def head(kind, u, **kw):
        return Step(kind, a=a, s=u // H, u=u, **kw)

    def group(kind, g):
        return Step(kind, a=a, s=g // a.groups, g=g)

    def maxima(u, t):
        out.append(head("max", u, t=t))
        if t == last_max:
            out.append(head("shift", u))
            if a.wide:
                late.append((k + 1, head("row", u)))
            elif u % a.heads == a.heads - 1:
                late.append((k + 1, group("rows", u // a.heads)))

    nmax = 1 if a.cross else QT
    last_max = nmax - 1
    k = -1
    if not a.cross:
        out.append(Step("ring", a=a))
    out.append(group("project", 0))
    if not a.wide:
        out.append(group("project", 1))
    for u in range(a.lead):
        for t in range(nmax):
            maxima(u, t)
        out += [st for _, st in late]
        late.clear()
    if a.wide:
        out.append(group("project", 1))
    slots = [(u, t) for u in range(nh) for t in range(nt)]
    lag = 2
    fills = [list(fill0), []]
    second = False
    for k in range(len(slots) + lag):
        if k < len(slots):
            u, t = slots[k]
            if t == 0 and u % a.heads == 0 and u // a.heads + 2 < ng:
                g2 = u // a.heads + 2
                if g2 >= a.groups and fills[0]:
                    out += fills[0]
                    fills[0] = []
                out.append(group("project", g2))
            out.append(head("scores", u, t=t))
            if u + a.lead < nh:
                maxima(u + a.lead, t)
        if k >= lag:
            u, t = slots[k - lag]
            out.append(head("values", u, t=t))
            if t == nt - 1 and u % a.heads == a.heads - 1:
                g = u // a.heads
                late.append((k if a.wide else k + 1, group("norm", g)))
                late.append((k + 2, group("out", g)))
        due = [st for at, st in late if at <= k]
        late = [(at, st) for at, st in late if at > k]
        for st in due:
            out.append(st)
            if st.kind == "out" and st.g == a.groups - 1:
                fills[1] = list(fill1)
        per = 1 if not a.cross else 2
        for f in fills:
            for _ in range(per):
                if f:
                    out.append(f.pop(0))
                    while f and out[-1].kind == f[0].kind == "up":
                        out.append(f.pop(0))
    out += [st for _, st in sorted(late, key=lambda x: x[0])]
    if any(st.kind == "out" and st.g == a.groups - 1 for _, st in late):
        fills[1] = list(fill1)
    return out + fills[0] + fills[1]


def make_plan():
    plan = dense_before(ATTENTIONS[0], 0)
    for n, a in enumerate(ATTENTIONS):
        before = feed_forward(a.layer - 1, 1) if n and not a.cross else []
        fill0 = before + dense_before(a, 1)
        after = feed_forward(a.layer, 0) if a.cross else []
        fill1 = after + (dense_before(ATTENTIONS[n + 1], 0) if n + 1 < len(ATTENTIONS) else [])
        plan += attention_steps(a, fill0, fill1)
    return plan + feed_forward(3, 1)


def number(plan):
    at, bank, kinds = {}, 0, {}
    split = 0
    for st in plan:
        st.bank = bank
        kind = {"mean": "ln"}.get(st.kind, st.kind)
        if st.kind == "var":
            st.n = kinds["ln"] - 1
            at["ln", st.s, st.ln] = st.n
        else:
            st.n = kinds.get(kind, 0)
            kinds[kind] = st.n + 1
        if st.kind in ("mean", "var", "v", "row", "rows", "out", "down"):
            bank += 1
        if st.kind == "up":
            bank += 2 if st.layer in (1, 2) else 1
        if st.kind == "project":
            bank += 4 if st.a.rope else 2
            st.split = split
            split += 2
            if st.a.wide:
                st.n_wide = kinds["wide"] = kinds.get("wide", -1) + 1
        if st.kind == "v":
            at["v", st.s, st.a.name] = st.bank
        if st.kind == "row":
            at["row", st.a.name, st.u] = st.bank
            at["row_n", st.n] = st.bank
        if st.kind == "rows":
            for j in range(4):
                at["row", st.a.name, st.g * 4 + j] = st.bank
        if st.kind == "shift":
            at["shift", st.a.name, st.u] = st.n
            at["shift_n", st.n] = (st.a.name, st.u)
        if st.kind == "project":
            at["project", st.a.name, st.g] = st
        if st.kind == "scores":
            at["scores", st.a.name, st.u, st.t] = st.n
        if st.kind == "norm":
            at["norm", st.a.name, st.g] = st.n
            at["norm_n", st.n] = st
            if not st.a.wide:
                st.narrow = kinds["narrow"] = kinds.get("narrow", -1) + 1
        if st.kind in ("out", "down"):
            at["x", st.s] = st.bank
        if st.kind in ("mean", "out", "down"):
            st.x = at.get(("x_was", st.s))
        if st.kind in ("out", "down"):
            at["x_was", st.s] = st.bank
            if st.kind == "out":
                at["out", st.a.name, st.g] = st.bank
            else:
                at["down", st.layer, st.s] = st.bank
        if st.kind == "max":
            at["max", st.a.name, st.u] = st.n
        if st.kind == "values":
            at["values", st.a.name, st.u] = st.n
        if st.kind == "ring":
            at["ring", st.a.layer] = st.n
            st.after = kinds.get("scores", 0)
    return at


def build(nc, x_in, ctx_in, cond_in, vec_in, ident_in, mod_w_in, mod_b_in, cond_w_in, kept_in,
          self0_in, cross0_in, self2_in, cross2_in, out):
    plan = make_plan()
    at = number(plan)
    with ExitStack() as ctx:
        def sb(name, shape, dt=F32):
            return ctx.enter_context(nc.sbuf_tensor(name, shape, dt))

        def sem(name):
            return ctx.enter_context(nc.semaphore(name))

        kept = sb("kept", [P, KEPT_N])
        wide_self, wide_cross = sb("wide_self", [P, WIDE_N]), sb("wide_cross", [P, WIDE_N])
        vec, mod_b = sb("vec", [P, len(VECS)]), sb("mod_b", [P, NM])
        ident = sb("ident", [P, P], BF16)
        mods, cur = sb("mods", [P, len(MODS), B]), sb("cur", [P, len(MODS), SLOTS])
        cond, silu = sb("cond", [P, B]), sb("silu", [P, B])
        ctx_all, ctx_cur = sb("ctx_all", [P, 4, B * NC]), sb("ctx_cur", [P, 4, SLOTS * NC])
        xs, hs = sb("xs", [P, SLOTS, N]), sb("hs", [P, SLOTS, N])
        centred, squared, rstd = sb("centred", [P, N]), sb("squared", [P, N]), sb("rstd", [P, N])
        vs = sb("vs", [P, SLOTS, QT, 1024])
        ring = sb("ring", [P, 3, 8, N], BF16)
        his, los = sb("his", [P, 2, N], BF16), sb("los", [P, 2, N], BF16)
        rope_a, rope_b = sb("rope_a", [P, N]), sb("rope_b", [P, N])
        shift_parts = sb("shift_parts", [P, 4, QT, 32], BF16)
        neg_max = sb("neg_max", [P, 4, QT])
        probs = sb("probs", [P, 3, N])
        heads_out, recip, unnormed = sb("heads_out", [P, 2, N]), sb("recip", [P, N]), sb("unnormed", [P, N])
        hidden = sb("hidden", [P, FC, N])

        general = [ctx.enter_context(nc.psum_tensor(f"general{i}", [P, N], F32)) for i in range(2)]
        max_bank = [ctx.enter_context(nc.psum_tensor(f"max_bank{i}", [P, N], F32)) for i in range(2)]
        score_bank = [ctx.enter_context(nc.psum_tensor(f"score_bank{i}", [P, N], F32)) for i in range(2)]
        value_bank = ctx.enter_context(nc.psum_tensor("value_bank", [P, N], F32))
        denom_bank = ctx.enter_context(nc.psum_tensor("denom_bank", [P, N], F32))

        def w(name, lo=0, n=None):
            first, width = KEPT_AT[name]
            return kept[:, first + lo:first + lo + (width if n is None else n)]

        def wide(a, name, lo, n):
            first = WIDE_AT[name][0] + lo
            return (wide_cross if a.cross else wide_self)[:, first:first + n]

        def v_col(name):
            return vec[:, VEC[name]:VEC[name] + 1]

        def mod(name, s):
            return cur[:, MOD[name], s:s + 1]

        def load_exp_ln():
            nc.scalar.add_instruction(mybir.InstLoadActFuncSet(
                act_func_set_id=EXP_LN_SET, name=nc.get_next_instruction_name(),
                engine=mybir.EngineType.Activation))

        loaded, const_loaded = sem("loaded"), sem("const_loaded")
        setup_vector, setup_scalar, setup_tensor, setup_pool = (
            sem("setup_vector"), sem("setup_scalar"), sem("setup_tensor"), sem("setup_pool"))

        staging = ring[:, :, :, :].rearrange("p r k n -> p (r k n)").bitcast(F32)
        mod_w = staging[:, 0:NM * P]
        cond_w = staging[:, NM * P:(NM + 2) * P]
        NK4 = B * NC

        with nc.Block() as block:
            @block.sync
            def _(sp):
                sp.dma_start(cond[:], cond_in).then_inc(const_loaded, 16)
                sp.dma_start(vec[:], vec_in).then_inc(const_loaded, 16)
                sp.dma_start(mod_b[:], mod_b_in).then_inc(const_loaded, 16)
                sp.dma_start(mod_w, mod_w_in).then_inc(const_loaded, 16)
                sp.dma_start(cond_w, cond_w_in).then_inc(const_loaded, 16)
                sp.dma_start(ident[:], ident_in).then_inc(const_loaded, 16)
                sp.wait_ge(setup_vector, 1)
                sp.dma_start(ctx_all[0:DC, 0, :], ctx_in).then_inc(const_loaded, 16)
                sp.dma_start(ctx_all[0:DC, 1, :], ctx_in).then_inc(const_loaded, 16)
                sp.dma_start(kept[:], kept_in).then_inc(loaded, 16)
                sp.wait_ge(const_loaded, 8 * 16)
                sp.wait_ge(loaded, 16)

            @block.gpsimd
            def _(pool):
                nc.gpsimd.memset(shift_parts[:], 0.0).then_inc(setup_pool, 1)
                nc.gpsimd.memset(recip[:], 1.0 / DC).then_inc(setup_pool, 1)
                pool.wait_ge(setup_pool, 2)

            @block.vector
            def _(dve):
                nc.vector.memset(ctx_all[:], 0.0).then_inc(setup_vector, 1)
                dve.wait_ge(setup_scalar, 1)
                nc.vector.tensor_scalar(silu[:], silu[:], 1.0, None, ALU.add).then_inc(setup_vector, 1)
                dve.wait_ge(setup_vector, 2)
                nc.vector.reciprocal(silu[:], silu[:]).then_inc(setup_vector, 1)
                dve.wait_ge(setup_vector, 3)
                nc.vector.tensor_tensor(silu[:], silu[:], cond[:], ALU.mult).then_inc(setup_vector, 1)
                dve.wait_ge(setup_tensor, 1)
                raw = general[0][:, 0:NM * B].rearrange("p (m b) -> p m b", b=B)
                nc.vector.tensor_tensor(mods[:, 0:NM, :], raw, mod_b[:].unsqueeze(2).broadcast_to([P, NM, B]),
                                        ALU.add).then_inc(setup_vector, 1)
                dve.wait_ge(setup_vector, 5)
                ns = len(MOD_SCALES)
                nc.vector.tensor_scalar(mods[:, 0:ns, :], mods[:, 0:ns, :], 1.0, None,
                                        ALU.add).then_inc(setup_vector, 1)
                dve.wait_ge(setup_vector, 6)
                for i, (g, b, lw, lb) in enumerate((("L0g1", "L0b1", "lw1", "lb1"), ("L0g2", "L0b2", "lw2", "lb2"))):
                    nc.vector.tensor_scalar(mods[:, MOD[f"L0A{i + 1}"], :], mods[:, MOD[g], :], v_col(lw), None,
                                            ALU.mult).then_inc(setup_vector, 1)
                    nc.vector.scalar_tensor_tensor(mods[:, MOD[f"L0B{i + 1}"], :], mods[:, MOD[g], :], v_col(lb),
                                                   mods[:, MOD[b], :], ALU.mult, ALU.add).then_inc(setup_vector, 1)
                nc.vector.tensor_scalar(mods[:, MOD["L1gb_ca"], :], mods[:, MOD["L1ga_ca"], :], v_col("L1bo_ca"),
                                        None, ALU.mult).then_inc(setup_vector, 1)
                dve.wait_ge(setup_tensor, 2)
                nc.vector.tensor_tensor(hidden[:, 0, 0:NK4], ctx_all[:, 0, :], general[1][:, 0:NK4],
                                        ALU.subtract).then_inc(setup_vector, 1)
                dve.wait_ge(setup_scalar, 4)
                nc.vector.tensor_tensor(hidden[:, 2, 0:NK4], hidden[:, 0, 0:NK4], hidden[:, 3, 0:NK4],
                                        ALU.mult).then_inc(setup_vector, 1)
                dve.wait_ge(setup_vector, 13)
                nc.vector.tensor_scalar(ctx_all[:, 0, :], hidden[:, 2, 0:NK4], v_col("cw"), v_col("cb"),
                                        ALU.mult, ALU.add).then_inc(setup_vector, 1)
                dve.wait_ge(setup_vector, 14)

            @block.scalar
            def _(act):
                load_exp_ln()
                act.wait_ge(const_loaded, 8 * 16)
                nc.scalar.activation(silu[:], cond[:], ACT.Exp, scale=-1.0).then_inc(setup_scalar, 1)
                act.wait_ge(setup_vector, 12)
                nc.scalar.activation(hidden[:, 1, 0:NK4], hidden[:, 0, 0:NK4], ACT.Square).then_inc(setup_scalar, 1)
                act.wait_ge(setup_tensor, 3)
                nc.scalar.activation(hidden[:, 2, 0:NK4], general[1][:, 0:NK4], ACT.Ln,
                                     bias=v_col("eps5")).then_inc(setup_scalar, 1)
                act.wait_ge(setup_scalar, 3)
                nc.scalar.activation(hidden[:, 3, 0:NK4], hidden[:, 2, 0:NK4], ACT.Exp, scale=-0.5)\
                    .then_inc(setup_scalar, 1)
                act.wait_ge(setup_tensor, 4)
                nc.scalar.activation(ctx_all[:, 2, :], max_bank[0][:, 0:NK4], ACT.Identity,
                                     bias=v_col("L1cond_b")).then_inc(setup_scalar, 1)
                nc.scalar.activation(ctx_all[:, 3, :], max_bank[1][:, 0:NK4], ACT.Identity,
                                     bias=v_col("L3b_ctx")).then_inc(setup_scalar, 1)
                act.wait_ge(setup_scalar, 6)

            @block.tensor
            def _(pe):
                pe.wait_ge(const_loaded, 8 * 16)
                pe.wait_ge(setup_vector, 4)
                for i, name in enumerate(MOD_SCALES + MOD_REST):
                    moving = silu if name[:2] in ("L1", "L3") else cond
                    last = nc.tensor.matmul(general[0][:, i * B:(i + 1) * B], mod_w[:, i * P:(i + 1) * P],
                                            moving[:], start=True, stop=True)
                last.then_inc(setup_tensor, 1)
                pe.wait_ge(setup_pool, 2)
                nc.tensor.matmul(general[1][:, 0:NK4], recip[:, 0:P], ctx_all[:, 0, :], start=True,
                                 stop=True).then_inc(setup_tensor, 1)
                pe.wait_ge(setup_scalar, 2)
                nc.tensor.matmul(general[1][:, 0:NK4], recip[0:DC, 0:P], hidden[0:DC, 1, 0:NK4], start=True,
                                 stop=True).then_inc(setup_tensor, 1)
                for i in range(2):
                    last = nc.tensor.matmul(max_bank[i][:, 0:NK4], cond_w[:, i * P:(i + 1) * P],
                                            ctx_all[:, 1, :], start=True, stop=True)
                last.then_inc(setup_tensor, 1)

        names = ("bank_filled bank_done0 bank_done1 max_filled max_reduced shift_split scores_filled probs_ready "
                 "values_done hi_ready split_done rope_products rope_sum shift_cleared ring_set unnormed_ready "
                 "denom_filled recip_ready heads_ready squares_ready rstd_ready normed_ready h_ready qk_ready "
                 "vector_chain scalar_chain pool_chain slots_ready x_loaded self_loaded cross_loaded stored "
                 "").split()
        sems = {n: sem(n) for n in names}
        bank_filled, max_filled, max_reduced = sems["bank_filled"], sems["max_filled"], sems["max_reduced"]
        bank_done = [sems["bank_done0"], sems["bank_done1"]]
        shift_split, scores_filled, probs_ready = sems["shift_split"], sems["scores_filled"], sems["probs_ready"]
        values_done, hi_ready, split_done = sems["values_done"], sems["hi_ready"], sems["split_done"]
        rope_products, rope_sum, shift_cleared = sems["rope_products"], sems["rope_sum"], sems["shift_cleared"]
        ring_set, unnormed_ready, denom_filled = sems["ring_set"], sems["unnormed_ready"], sems["denom_filled"]
        recip_ready, heads_ready, squares_ready = sems["recip_ready"], sems["heads_ready"], sems["squares_ready"]
        rstd_ready, normed_ready, h_ready = sems["rstd_ready"], sems["normed_ready"], sems["h_ready"]
        vector_chain, scalar_chain, pool_chain = sems["vector_chain"], sems["scalar_chain"], sems["pool_chain"]
        slots_ready, x_loaded = sems["slots_ready"], sems["x_loaded"]
        self_loaded, cross_loaded, stored = sems["self_loaded"], sems["cross_loaded"], sems["stored"]

        def bank_at(i):
            return general[i % 2]

        def wait_bank_free(eng, i):
            if i >= 2:
                eng.wait_ge(bank_done[i % 2], i // 2)

        def wait_bank_done(eng, i):
            eng.wait_ge(bank_done[i % 2], i // 2 + 1)

        def wait_x(eng, st):
            if st.x is None:
                eng.wait_ge(x_loaded, 16 * SLOTS)
            else:
                wait_bank_done(eng, st.x)

        def source(a, s, w_):
            if w_ == "k" and a.cross:
                kind = {0: 0, 2: 1, 1: 2, 3: 3}[a.layer]
                return ctx_cur[:, kind, s * NC:(s + 1) * NC]
            if a.layer == 1 and not a.cross:
                return vs[:, s, 0 if w_ == "q" else 1, 512:1024]
            return hs[:, s, :]

        def wait_source(eng, a, s):
            eng.wait_ge(h_ready, at["ln", s, (a.layer, int(a.cross))] + 1)
            if a.layer == 1 and not a.cross:
                eng.wait_ge(h_ready, at["ln", s, (1, "qk")] + 1)

        def wait_weights(eng, a):
            if a.wide:
                eng.wait_ge(cross_loaded if a.cross else self_loaded, 16 * (1 + a.layer // 2))

        def ring_of(g):
            return ring[:, g % 3]

        def ring_count(a):
            return 3 * (at["ring", a.layer] + 1)

        def has_bias(a):
            return a.name in ("L1c", "L3s")

        def first_scores(a):
            return at["scores", a.name, 0, 0]

        def max_count(a, u):
            return at["max", a.name, u] + 1

        def values_count(a, g):
            return at["values", a.name, (g + 1) * a.heads - 1] + 1

        def wait_output_banks_free(pe, a, n):
            if n:
                old = at["norm_n", n - 1]
                if old.a.wide or a.wide:
                    pe.wait_ge(heads_ready, n)
                else:
                    pe.wait_ge(unnormed_ready, old.narrow + 1)

        def up_weights(st):
            if st.layer == 1:
                return [w("L1w1", st.c * P, P), w("L1w3", st.c * P, P)]
            if st.layer == 2:
                return [w("L2ff1", FF + st.c * P, P), w("L2ff1", st.c * P, P)]
            return [w(f"L{st.layer}ff1", st.c * P, P)]


        with nc.Fori(0, B // SLOTS) as pair:
            with nc.Block() as block:
                @block.sync
                def _(sp):
                    for s in range(SLOTS):
                        sp.dma_start(xs[:, s, :], x_in[:, bass.ds((pair * SLOTS + s) * N, N)]).then_inc(x_loaded, 16)
                    sp.dma_start(wide_self[:], self0_in).then_inc(self_loaded, 16)
                    sp.dma_start(wide_cross[:], cross0_in).then_inc(cross_loaded, 16)
                    for a, tile, src, landed in ((ATTENTIONS[0], wide_self, self2_in, self_loaded),
                                                 (ATTENTIONS[1], wide_cross, cross2_in, cross_loaded)):
                        wait_bank_done(sp, at["out", a.name, SLOTS * a.groups - 1])
                        sp.dma_start(tile[:, 0:WIDE2_N], src).then_inc(landed, 16)
                    for s in range(SLOTS):
                        wait_bank_done(sp, at["down", 3, s])
                        sp.dma_start(out[:, bass.ds((pair * SLOTS + s) * N, N)], xs[:, s, :]).then_inc(stored, 16)
                    sp.wait_ge(stored, 16 * SLOTS)

                @block.tensor
                def _(pe):
                    pe.wait_ge(slots_ready, 2)
                    for st in plan:
                        a = st.a
                        i = st.bank
                        if st.kind == "mean":
                            if st.head_norm:
                                pe.wait_ge(h_ready, at["ln", st.s, (1, 0)] + 1)
                            else:
                                wait_x(pe, st)
                            wait_bank_free(pe, i)
                            src = hs[:, st.s, :] if st.head_norm else xs[:, st.s, :]
                            nc.tensor.matmul(bank_at(i)[:], w("avg8" if st.head_norm else "avg"), src,
                                             start=True, stop=True).then_inc(bank_filled, 1)
                        elif st.kind == "var":
                            pe.wait_ge(squares_ready, st.n + 1)
                            wait_bank_free(pe, i)
                            nc.tensor.matmul(bank_at(i)[:], w("avg8" if st.head_norm else "avg"), squared[:],
                                             start=True, stop=True).then_inc(bank_filled, 1)
                        elif st.kind == "v":
                            pe.wait_ge(h_ready, at["ln", st.s, (a.layer, int(a.cross))] + 1)
                            wait_weights(pe, a)
                            wait_bank_free(pe, i)
                            n = a.tiles[st.t]
                            src = source(a, st.s, "k") if a.cross else hs[:, st.s, st.t * P:(st.t + 1) * P]
                            if a.wide:
                                right = wide(a, "v", st.c * 512, 512)
                            else:
                                right = w("pick_v" if a.name == "L1s" else a.name + "_v")
                            nc.tensor.matmul(bank_at(i)[0:n, :], src, right, start=True, stop=True)\
                                .then_inc(bank_filled, 1)
                        elif st.kind == "project":
                            wait_source(pe, a, st.s)
                            wait_weights(pe, a)
                            g = st.g % a.groups
                            for part in "qk":
                                src = source(a, st.s, part)
                                n = src.shape[-1]
                                for swapped in range(1 + a.rope):
                                    if a.wide:
                                        left = wide(a, part + "s" * swapped, g * P, P)
                                    elif a.name == "L1s":
                                        left = w("pick_qk", g * P, P)
                                    else:
                                        left = w(f"{a.name}_{part}", g * P, P)
                                    wait_bank_free(pe, i)
                                    nc.tensor.matmul(bank_at(i)[:, 0:n], left, src, start=True, stop=True)\
                                        .then_inc(bank_filled, 1)
                                    i += 1
                        elif st.kind == "max":
                            g, j = st.u // a.heads, st.u % a.heads
                            st_project = at["project", a.name, g]
                            if st.t == 0 and (j == 0):
                                pe.wait_ge(split_done, st_project.split + 2)
                                if a.wide:
                                    pe.wait_ge(shift_cleared, st_project.n_wide + 1)
                                if st.u == 0:
                                    pe.wait_ge(ring_set, ring_count(a))
                            if st.n >= 2:
                                pe.wait_ge(max_reduced, st.n - 1)
                            r, bank, nk = ring_of(g), max_bank[st.n % 2], a.keys
                            for q in (range(QT) if a.cross else (st.t,)):
                                to = bank[:, q * nk:(q + 1) * nk] if a.cross else bank[:]
                                lo, hi = q * P, (q + 1) * P
                                if a.wide:
                                    nc.tensor.matmul(to, r[:, 4 * j, lo:hi], r[:, 4 * j + 2, 0:nk],
                                                     start=True, stop=False)
                                    last = nc.tensor.matmul(to, r[:, 4 * j + 1, lo:hi], r[:, 4 * j + 3, 0:nk],
                                                            start=False, stop=True)
                                else:
                                    last = nc.tensor.matmul(to, r[:, 0, lo:hi], r[:, 1 + j, 0:nk],
                                                            start=True, stop=True)
                            last.then_inc(max_filled, 1)
                        elif st.kind == "row":
                            pe.wait_ge(shift_split, at["shift", a.name, st.u] + 1)
                            wait_bank_free(pe, i)
                            m = at["shift", a.name, st.u] % 4
                            for q in range(QT):
                                last = nc.tensor.matmul(bank_at(i)[64:96, q * P:(q + 1) * P],
                                                        shift_parts[:, m, q, :], ident[:], start=True, stop=True)
                            last.then_inc(bank_filled, 1)
                        elif st.kind == "rows":
                            pe.wait_ge(shift_split, at["shift", a.name, 4 * st.g + 3] + 1)
                            wait_bank_free(pe, i)
                            for j in range(4):
                                m = at["shift", a.name, 4 * st.g + j] % 4
                                for q in range(QT):
                                    last = nc.tensor.matmul(
                                        bank_at(i)[32 * j:32 * j + 32, q * P:(q + 1) * P],
                                        shift_parts[:, m, q, :], ident[:], start=True, stop=True)
                            last.then_inc(bank_filled, 1)
                        elif st.kind == "scores":
                            g, j = st.u // a.heads, st.u % a.heads
                            if st.t == 0:
                                wait_bank_done(pe, at["row", a.name, st.u])
                            if st.n >= 2:
                                pe.wait_ge(probs_ready, st.n - 1)
                            r, bank, nk = ring_of(g), score_bank[st.n % 2], a.tiles[st.t]
                            lo = st.t * P
                            if a.wide:
                                nc.tensor.matmul(bank[0:nk, :], r[:, 4 * j + 2, lo:lo + nk], r[:, 4 * j, :],
                                                 start=True, stop=False)
                                last = nc.tensor.matmul(bank[0:nk, :], r[:, 4 * j + 3, lo:lo + nk],
                                                        r[:, 4 * j + 1, :], start=False, stop=True)
                            else:
                                last = nc.tensor.matmul(bank[0:nk, :], r[:, 1 + j, lo:lo + nk], r[:, 0, :],
                                                        start=True, stop=True)
                            last.then_inc(scores_filled, 1)
                        elif st.kind == "values":
                            j, h = st.u % a.heads, st.u % H
                            n, nk = at["scores", a.name, st.u, st.t], a.tiles[st.t]
                            first, last_tile = st.t == 0, st.t == len(a.tiles) - 1
                            if st.u % H == 0 and first:
                                last_v = at["v", st.s, a.name]
                                wait_bank_done(pe, last_v)
                                if last_v:
                                    wait_bank_done(pe, last_v - 1)
                            if j == 0 and first:
                                norm = at["norm", a.name, st.u // a.heads]
                                wait_output_banks_free(pe, a, norm)
                            pe.wait_ge(probs_ready, n + 1)
                            prob = probs[0:nk, n % 3, :]
                            if a.wide:
                                nc.tensor.matmul(value_bank[64 * j:64 * j + 64, :],
                                                 vs[0:nk, st.s, st.t, h * 64:(h + 1) * 64], prob,
                                                 start=first, stop=last_tile)
                                last = nc.tensor.matmul(denom_bank[64 * j:64 * j + 64, :], w("ones")[0:nk, :], prob,
                                                        start=first, stop=last_tile)
                            else:
                                last = nc.tensor.matmul(value_bank[32 * j:32 * j + 32, :],
                                                        vs[0:nk, st.s, st.t, h * 32:(h + 1) * 32], prob,
                                                        start=first, stop=last_tile)
                            last.then_inc(values_done, 1)
                        elif st.kind == "norm" and not a.wide:
                            pe.wait_ge(unnormed_ready, st.narrow + 1)
                            if st.n >= 1:
                                pe.wait_ge(recip_ready, st.n)
                            nc.tensor.matmul(denom_bank[:], w("dsel"), unnormed[:], start=True, stop=True)\
                                .then_inc(denom_filled, 1)
                        elif st.kind == "out":
                            pe.wait_ge(heads_ready, at["norm", a.name, st.g] + 1)
                            wait_bank_free(pe, i)
                            g = st.g % a.groups
                            left = wide(a, "wo", g * P, P) if a.wide else w(a.name + "_wo", g * P, P)
                            nc.tensor.matmul(bank_at(i)[:], left, heads_out[:, at["norm", a.name, st.g] % 2, :],
                                             start=True, stop=True).then_inc(bank_filled, 1)
                        elif st.kind == "up":
                            pe.wait_ge(h_ready, at["ln", st.s, (st.layer, 2)] + 1)
                            for left in up_weights(st):
                                wait_bank_free(pe, i)
                                nc.tensor.matmul(bank_at(i)[:], left, hs[:, st.s, :], start=True, stop=True)\
                                    .then_inc(bank_filled, 1)
                                i += 1
                        elif st.kind == "down":
                            wait_bank_free(pe, i)
                            wait_bank_done(pe, i - 1)
                            if st.layer in (0, 3):
                                wait_bank_done(pe, i - 2)
                            name = {0: "L0ff2", 1: "L1w2", 2: "L2ff2", 3: "L3ff2"}[st.layer]
                            for c in range(FC):
                                last = nc.tensor.matmul(bank_at(i)[:], w(name, c * P, P), hidden[:, c, :],
                                                        start=c == 0, stop=c == FC - 1)
                            last.then_inc(bank_filled, 1)

                @block.scalar
                def _(act):
                    chain = [0]

                    def link(ins):
                        chain[0] += 1
                        ins.then_inc(scalar_chain, 1)
                        act.wait_ge(scalar_chain, chain[0])

                    load_exp_ln()
                    act.wait_ge(slots_ready, 2)
                    for st in plan:
                        a = st.a
                        i = st.bank
                        if st.kind == "mean":
                            wait_bank_done(act, i)
                            nc.scalar.activation(squared[:], centred[:], ACT.Square).then_inc(squares_ready, 1)
                        elif st.kind == "var":
                            act.wait_ge(bank_filled, i + 1)
                            if st.n >= 1:
                                act.wait_ge(normed_ready, st.n)
                            eps = "eps6" if st.head_norm else LN_EPS[st.ln[0]]
                            nc.scalar.activation(rstd[:], bank_at(i)[:], ACT.Ln, bias=v_col(eps))\
                                .then_inc(bank_done[i % 2], 1)
                            wait_bank_done(act, i)
                            nc.scalar.activation(rstd[:], rstd[:], ACT.Exp, scale=-0.5).then_inc(rstd_ready, 1)
                            act.wait_ge(normed_ready, st.n + 1)
                            if st.head_norm:
                                nc.scalar.activation(vs[:, st.s, 0, 512:1024], centred[:], ACT.Identity,
                                                     scale=v_col("qn_w"), bias=v_col("qn_b"))
                                nc.scalar.activation(vs[:, st.s, 1, 512:1024], centred[:], ACT.Identity,
                                                     scale=v_col("kn_w"), bias=v_col("kn_b")).then_inc(h_ready, 1)
                            else:
                                scale, shift = LN_MODS[st.ln]
                                nc.scalar.activation(hs[:, st.s, :], centred[:], ACT.Identity,
                                                     scale=mod(scale, st.s), bias=mod(shift, st.s))\
                                    .then_inc(h_ready, 1)
                        elif st.kind == "v" and a.wide:
                            act.wait_ge(bank_filled, i + 1)
                            n = a.tiles[st.t]
                            nc.scalar.activation(vs[0:n, st.s, st.t, st.c * 512:(st.c + 1) * 512],
                                                 bank_at(i)[0:n, :], ACT.Identity).then_inc(bank_done[i % 2], 1)
                        elif st.kind == "project":
                            for p_, part in enumerate("qk"):
                                n = a.keys if part == "k" else N
                                sp_ = st.split + p_
                                if sp_ >= 2:
                                    act.wait_ge(split_done, sp_ - 1)
                                if a.rope:
                                    act.wait_ge(rope_sum, st.split + p_ + 1)
                                    nc.scalar.activation(his[:, sp_ % 2, 0:n], rope_a[:, 0:n], ACT.Identity)\
                                        .then_inc(hi_ready, 1)
                                    continue
                                act.wait_ge(bank_filled, i + 1)
                                if a.wide:
                                    nc.scalar.activation(his[:, sp_ % 2, 0:n], bank_at(i)[:, 0:n], ACT.Identity)\
                                        .then_inc(hi_ready, 1)
                                else:
                                    bias = v_col(f"{a.name}_b{part}m_{st.g % a.groups}") if has_bias(a) else 0.0
                                    nc.scalar.activation(his[:, sp_ % 2, 0:n], bank_at(i)[:, 0:n], ACT.Identity,
                                                         scale=v_col(part + "mask"), bias=bias).then_inc(hi_ready, 1)
                                i += 1
                        elif st.kind == "row":
                            act.wait_ge(bank_filled, i + 1)
                            g, j = st.u // a.heads, st.u % a.heads
                            nc.scalar.activation(ring_of(g)[64:96, 4 * j + 1, :], bank_at(i)[64:96, :],
                                                 ACT.Identity).then_inc(bank_done[i % 2], 1)
                        elif st.kind == "scores":
                            nk = a.tiles[st.t]
                            act.wait_ge(scores_filled, st.n + 1)
                            if st.n >= 3:
                                act.wait_ge(values_done, st.n - 2)
                            nc.scalar.activation(probs[0:nk, st.n % 3, :], score_bank[st.n % 2][0:nk, :], ACT.Exp,
                                                 scale=a.scale).then_inc(probs_ready, 1)
                        elif st.kind == "norm":
                            if st.n >= 1:
                                act.wait_ge(heads_ready, st.n)
                            if a.wide:
                                act.wait_ge(values_done, values_count(a, st.g))
                            else:
                                act.wait_ge(values_done, values_count(a, st.g))
                                nc.scalar.activation(unnormed[:], value_bank[:], ACT.Identity)\
                                    .then_inc(unnormed_ready, 1)
                                act.wait_ge(denom_filled, st.narrow + 1)
                            link(nc.scalar.activation(recip[:], denom_bank[:], ACT.Ln))
                            nc.scalar.activation(recip[:], recip[:], ACT.Exp, scale=-1.0).then_inc(recip_ready, 1)
                        elif st.kind == "up":
                            func = {0: ACT.Gelu, 1: ACT.Silu, 2: ACT.Gelu, 3: ACT.Gelu_apprx_tanh}[st.layer]
                            bias = {0: f"L0ff_b1_{st.c}", 2: f"L2ff_g_{st.c}", 3: f"L3ff_b1_{st.c}"}
                            act.wait_ge(bank_filled, i + 1)
                            nc.scalar.activation(hidden[:, st.c, :], bank_at(i)[:], func,
                                                 bias=v_col(bias[st.layer]) if st.layer in bias else 0.0)\
                                .then_inc(bank_done[i % 2], 1)
                            if st.c == FC - 1:
                                load_exp_ln()

                @block.vector
                def _(dve):
                    chain = [0]

                    def link(ins):
                        chain[0] += 1
                        ins.then_inc(vector_chain, 1)
                        dve.wait_ge(vector_chain, chain[0])

                    nc.vector.tensor_copy(cur[:], mods[:, :, bass.ds(pair * SLOTS, SLOTS)]).then_inc(slots_ready, 1)
                    nc.vector.tensor_copy(ctx_cur[:], ctx_all[:, :, bass.ds(pair * (SLOTS * NC), SLOTS * NC)])\
                        .then_inc(slots_ready, 1)
                    for st in plan:
                        a = st.a
                        i = st.bank
                        if st.kind == "mean":
                            dve.wait_ge(bank_filled, i + 1)
                            if st.n >= 1:
                                dve.wait_ge(h_ready, st.n)
                            src = hs[:, st.s, :] if st.head_norm else xs[:, st.s, :]
                            nc.vector.tensor_tensor(centred[:], src, bank_at(i)[:], ALU.subtract)\
                                .then_inc(bank_done[i % 2], 1)
                        elif st.kind == "var":
                            dve.wait_ge(rstd_ready, st.n + 1)
                            nc.vector.tensor_tensor(centred[:], centred[:], rstd[:], ALU.mult)\
                                .then_inc(normed_ready, 1)
                        elif st.kind == "v" and not a.wide:
                            dve.wait_ge(bank_filled, i + 1)
                            n = a.tiles[st.t]
                            bias = w(a.name + "_bv" if a.name in ("L1c", "L3s") else "bv_ones")
                            nc.vector.tensor_tensor(vs[0:n, st.s, st.t, 0:512], bank_at(i)[0:n, :], bias[0:n, :],
                                                    ALU.add).then_inc(bank_done[i % 2], 1)
                        elif st.kind == "project":
                            r = ring_of(st.g)
                            if st.g >= 3:
                                u = (st.g - 2) * a.heads - 1
                                dve.wait_ge(scores_filled, at["scores", a.name, u, len(a.tiles) - 1] + 1)
                            elif not a.cross:
                                dve.wait_ge(ring_set, ring_count(a))
                            else:
                                dve.wait_ge(scores_filled, first_scores(a))
                            for p_, part in enumerate("qk"):
                                n = a.keys if part == "k" else N
                                sp_ = st.split + p_
                                if sp_ >= 2:
                                    dve.wait_ge(split_done, sp_ - 1)
                                hi, lo = his[:, sp_ % 2, 0:n], los[:, sp_ % 2, 0:n]
                                if a.rope:
                                    rc = st.split + p_
                                    if rc >= 1:
                                        dve.wait_ge(split_done, sp_)
                                        dve.wait_ge(hi_ready, sp_)
                                        dve.wait_ge(rope_sum, rc)
                                    dve.wait_ge(bank_filled, i + 1)
                                    nc.vector.tensor_tensor(rope_a[:, 0:n], bank_at(i)[:, 0:n], w("rope_c")[:, 0:n],
                                                            ALU.mult).then_inc(bank_done[i % 2], 1)
                                    i += 1
                                    dve.wait_ge(bank_filled, i + 1)
                                    nc.vector.tensor_tensor(rope_b[:, 0:n], bank_at(i)[:, 0:n], w("rope_s")[:, 0:n],
                                                            ALU.mult).then_inc(bank_done[i % 2], 1)
                                    i += 1
                                    dve.wait_ge(hi_ready, sp_ + 1)
                                    link(nc.vector.tensor_tensor(lo, rope_a[:, 0:n], hi, ALU.subtract))
                                elif a.wide:
                                    dve.wait_ge(hi_ready, sp_ + 1)
                                    nc.vector.tensor_tensor(lo, bank_at(i)[:, 0:n], hi, ALU.subtract)\
                                        .then_inc(bank_done[i % 2], 1)
                                    wait_bank_done(dve, i)
                                    i += 1
                                else:
                                    dve.wait_ge(hi_ready, sp_ + 1)
                                    if has_bias(a):
                                        bias = v_col(f"{a.name}_b{part}_{st.g % a.groups}")
                                    else:
                                        bias = v_col("kones") if part == "k" else 0.0
                                    to = r[:, 0, :] if part == "q" else lo
                                    nc.vector.scalar_tensor_tensor(to, bank_at(i)[:, 0:n], bias, hi, ALU.add,
                                                                   ALU.subtract).then_inc(bank_done[i % 2], 1)
                                    wait_bank_done(dve, i)
                                    i += 1
                                if a.wide:
                                    for j in range(2):
                                        rows = slice(64 * j, 64 * j + 64)
                                        if part == "q":
                                            nc.vector.tensor_copy(r[0:64, 4 * j, :], hi[rows, :])
                                            nc.vector.tensor_copy(r[64:128, 4 * j, :], hi[rows, :])
                                            last = nc.vector.tensor_copy(r[0:64, 4 * j + 1, :], lo[rows, :])
                                        else:
                                            nc.vector.tensor_copy(r[0:64, 4 * j + 2, 0:n], hi[rows, :])
                                            nc.vector.tensor_copy(r[0:64, 4 * j + 3, 0:n], hi[rows, :])
                                            last = nc.vector.tensor_copy(r[64:128, 4 * j + 2, 0:n], lo[rows, :])
                                    last.then_inc(split_done, 1)
                                elif part == "k":
                                    for j in range(4):
                                        rows = slice(32 * j, 32 * j + 32)
                                        last = nc.vector.tensor_copy(r[rows, 1 + j, 0:n], lo[rows, :])
                                    last.then_inc(split_done, 1)
                                else:
                                    dve.sem_inc(split_done, 1)
                        elif st.kind == "max":
                            nk = a.keys
                            dve.wait_ge(max_filled, st.n + 1)
                            m = at["shift", a.name, st.u] % 4
                            if a.cross:
                                src = max_bank[st.n % 2][:, 0:QT * nk].rearrange("p (q k) -> p q k", k=nk)
                                to = neg_max[:, m, :]
                            else:
                                src, to = max_bank[st.n % 2][:], neg_max[:, m, st.t:st.t + 1]
                            nc.vector.tensor_reduce(to, src, AXIS_X, ALU.max, negate=True).then_inc(max_reduced, 1)
                        elif st.kind == "shift":
                            m = st.n % 4
                            dve.wait_ge(max_reduced, max_count(a, st.u))
                            if st.n >= 4:
                                name, u = at["shift_n", st.n - 4]
                                dve.wait_ge(bank_filled, at["row", name, u] + 1)
                            link(nc.vector.tensor_copy(shift_parts[:, m, :, 0], neg_max[:, m, :]))
                            nc.vector.tensor_tensor(shift_parts[:, m, :, 1], neg_max[:, m, :],
                                                    shift_parts[:, m, :, 0], ALU.subtract).then_inc(shift_split, 1)
                        elif st.kind == "rows":
                            dve.wait_ge(bank_filled, i + 1)
                            q = ring_of(st.g)[:, 0, :]
                            nc.vector.tensor_tensor(q, bank_at(i)[:], q, ALU.add).then_inc(bank_done[i % 2], 1)
                        elif st.kind == "norm":
                            dve.wait_ge(recip_ready, st.n + 1)
                            if st.n >= 2:
                                old = at["norm_n", st.n - 2]
                                dve.wait_ge(bank_filled, at["out", old.a.name, old.g] + 1)
                            nc.vector.tensor_tensor(heads_out[:, st.n % 2, :],
                                                    value_bank[:] if a.wide else unnormed[:], recip[:],
                                                    ALU.mult).then_inc(heads_ready, 1)
                        elif st.kind in ("out", "down"):
                            dve.wait_ge(bank_filled, i + 1)
                            wait_x(dve, st)
                            x = xs[:, st.s, :]
                            if st.kind == "out":
                                first = st.g % a.groups == 0
                                gate = {"L1s": "L1ga_sa", "L1c": "L1ga_ca"}.get(a.name)
                                bias = f"L{a.layer}bo_{'ca' if a.cross else 'sa'}"
                            else:
                                first, gate, bias = True, "L1ga_ff" if st.layer == 1 else None, f"L{st.layer}ff_b2"
                            if gate is not None:
                                if first and st.kind == "out" and a.cross:
                                    link(nc.vector.tensor_scalar(x, x, mod("L1gb_ca", st.s), None, ALU.add))
                                nc.vector.scalar_tensor_tensor(x, bank_at(i)[:], mod(gate, st.s), x, ALU.mult,
                                                               ALU.add).then_inc(bank_done[i % 2], 1)
                            elif first:
                                nc.vector.scalar_tensor_tensor(x, bank_at(i)[:], v_col(bias), x, ALU.add,
                                                               ALU.add).then_inc(bank_done[i % 2], 1)
                            else:
                                nc.vector.tensor_tensor(x, bank_at(i)[:], x, ALU.add).then_inc(bank_done[i % 2], 1)
                        elif st.kind == "up" and st.layer in (1, 2):
                            wait_bank_done(dve, i)
                            i += 1
                            dve.wait_ge(bank_filled, i + 1)
                            hid = hidden[:, st.c, :]
                            nc.vector.scalar_tensor_tensor(
                                hid, bank_at(i)[:], v_col(f"L2ff_a_{st.c}") if st.layer == 2 else 0.0, hid,
                                ALU.add, ALU.mult).then_inc(bank_done[i % 2], 1)

                @block.gpsimd
                def _(pool):
                    chain = [0]

                    def link(ins):
                        chain[0] += 1
                        ins.then_inc(pool_chain, 1)
                        pool.wait_ge(pool_chain, chain[0])

                    for st in plan:
                        a = st.a
                        if st.kind == "ring":
                            if st.after:
                                pool.wait_ge(scores_filled, st.after)
                            for r in range(3):
                                if a.wide:
                                    for j in range(2):
                                        link(nc.gpsimd.memset(ring[64:128, r, 4 * j + 3, :], 0.0))
                                        link(nc.gpsimd.memset(ring[64:66, r, 4 * j + 3, :], 1.0))
                                        last = nc.gpsimd.memset(ring[64:128, r, 4 * j + 1, :], 0.0)
                                else:
                                    last = nc.gpsimd.memset(ring[:, r, 1:5, :], 0.0)
                                last.then_inc(ring_set, 1)
                            pool.wait_ge(ring_set, ring_count(a))
                        elif st.kind == "project" and a.wide:
                            if st.g >= 3:
                                u = (st.g - 2) * a.heads - 1
                                pool.wait_ge(scores_filled, at["scores", a.name, u, len(a.tiles) - 1] + 1)
                            elif a.cross:
                                pool.wait_ge(scores_filled, first_scores(a))
                            else:
                                pool.wait_ge(ring_set, ring_count(a))
                            for j in range(2):
                                last = nc.gpsimd.memset(ring_of(st.g)[64:96, 4 * j + 1, :], 0.0)
                            last.then_inc(shift_cleared, 1)
                            pool.wait_ge(shift_cleared, st.n_wide + 1)
                            if a.rope:
                                for p_ in range(2):
                                    n = N if p_ == 0 else a.keys
                                    b0 = st.bank + 2 * p_
                                    wait_bank_done(pool, b0)
                                    wait_bank_done(pool, b0 + 1)
                                    nc.gpsimd.tensor_tensor(rope_a[:, 0:n], rope_a[:, 0:n], rope_b[:, 0:n], ALU.add)\
                                        .then_inc(rope_sum, 1)
                                    pool.wait_ge(rope_sum, st.split + p_ + 1)

            with nc.Block() as block:
                @block.gpsimd
                def _(pool):
                    for s in sems.values():
                        pool.sem_clear(s)


def rows128(m):
    return np.concatenate([m, np.zeros((P - m.shape[0], m.shape[1]), m.dtype)]) if m.shape[0] < P else m


def chunks(m):
    return m.reshape(-1, P, m.shape[1]).transpose(1, 0, 2).reshape(P, -1)


def head_blocks(m, copies):
    out = np.zeros((m.shape[0], H, 32), m.dtype)
    for c in copies:
        out[:, :, c:c + 8] = m.reshape(-1, H, 8)
    return out.reshape(m.shape[0], H * 32)


STACK = (8, 16, 24)
LOW_OF_Q, LOW_OF_K = 24, 16


def swap_pairs(m):
    return m.reshape(m.shape[0], -1, 2)[:, :, ::-1].reshape(m.shape)


def out_rows(m):
    out = np.zeros((4, 4, 32, P), m.dtype)
    out[:, :, 0:8, :] = m.reshape(4, 4, 8, P)
    return out.reshape(4, P, P).transpose(1, 0, 2).reshape(P, 4 * P)


def bias_groups(b, copies, ones=False):
    m = head_blocks(b.reshape(1, P), copies).reshape(4, P)
    if ones:
        m = m.copy()
        m.reshape(4, 4, 32)[:, :, 0:2] = 1.0
    return m


def kernel(**inputs):
    import concourse.bacc as bacc
    from concourse.bass_utils import run_bass_kernel_spmd

    I = {n: np.asarray(v) for n, v in inputs.items()}
    f32 = np.float32
    L0 = {n[9:]: v for n, v in I.items() if n.startswith("L0_xcond_")}
    L1 = {n[9:]: v for n, v in I.items() if n.startswith("L1_xcond_")}
    L2 = {n[9:]: v for n, v in I.items() if n.startswith("L2_xcond_")}
    L3 = {n[9:]: v for n, v in I.items() if n.startswith("L3_xcond_")}

    ada1 = L1["adaln_w"].T
    order1 = ["L1sh_sa", "L1sc_sa", "L1ga_sa", "L1sh_ca", "L1sc_ca", "L1ga_ca", "L1sh_ff", "L1sc_ff", "L1ga_ff"]
    order3 = ["L3sh_msa", "L3sc_msa", "L3sh_x", "L3sc_x", "L3sh_mlp", "L3sc_mlp"]
    mw = {"L0g1": (L0["g1_w"], L0["g1_b"]), "L0b1": (L0["b1_w"], L0["b1_b"]),
          "L0g2": (L0["g2_w"], L0["g2_b"]), "L0b2": (L0["b2_w"], L0["b2_b"])}
    for i, n in enumerate(order1):
        mw[n] = (ada1[:, i * P:(i + 1) * P], L1["adaln_b"][i * P:(i + 1) * P])
    for i in range(3):
        for j, n in enumerate((f"L2s{i + 1}", f"L2t{i + 1}")):
            mw[n] = (L2[f"n{i + 1}_w"][:, j * P:(j + 1) * P], L2[f"n{i + 1}_b"][j * P:(j + 1) * P])
    for i, n in enumerate(order3):
        mw[n] = (L3["W_ada"][:, i * P:(i + 1) * P], L3["b_ada"][i * P:(i + 1) * P])
    mod_w = np.concatenate([mw[n][0] for n in MOD_SCALES + MOD_REST], 1)
    mod_b = np.stack([mw[n][1] for n in MOD_SCALES + MOD_REST], 1)

    vec = {"eps5": np.full(P, 1e-5, f32), "eps6": np.full(P, 1e-6, f32),
           "lw1": L0["ln1_w"], "lb1": L0["ln1_b"], "lw2": L0["ln2_w"], "lb2": L0["ln2_b"],
           "cw": rows128(L0["ca_lnc_w"][:, None])[:, 0], "cb": rows128(L0["ca_lnc_b"][:, None])[:, 0],
           "L1cond_b": L1["cond_b"], "L3b_ctx": L3["b_ctx"], "L1bo_ca": L1["ca_out_b"],
           "L0bo_sa": L0["sa_bo"], "L0bo_ca": L0["ca_bo"], "L0ff_b2": L0["ff_b2"],
           "L2bo_sa": L2["o1_b"], "L2bo_ca": L2["o2_b"], "L2ff_b2": L2["ff_b2"],
           "L3bo_sa": L3["b_proj"], "L3bo_ca": L3["b_out"], "L3ff_b2": L3["b_fc2"]}
    for n in ("qn_w", "qn_b", "kn_w", "kn_b"):
        vec[n] = np.tile(L1[n], H)
    block = np.arange(P) % 32
    vec["qmask"] = (block >= LOW_OF_Q).astype(f32)
    vec["kmask"] = ((block >= LOW_OF_K) & (block < LOW_OF_K + 8)).astype(f32)
    vec["kones"] = (block < 2).astype(f32)
    for c in range(FC):
        sl = slice(c * P, (c + 1) * P)
        vec[f"L0ff_b1_{c}"], vec[f"L3ff_b1_{c}"] = L0["ff_b1"][sl], L3["b_fc1"][sl]
        vec[f"L2ff_a_{c}"], vec[f"L2ff_g_{c}"] = L2["ff_b1"][0:FF][sl], L2["ff_b1"][FF:][sl]
    for name, bias in (("L1c", L1["ca_in_b"]), ("L3s", L3["b_qkv"])):
        for i, part in enumerate("qk"):
            b = bias[i * P:(i + 1) * P]
            full = bias_groups(b, STACK, ones=part == "k")
            low = bias_groups(b, (LOW_OF_Q if part == "q" else LOW_OF_K,))
            for g in range(4):
                vec[f"{name}_b{part}_{g}"], vec[f"{name}_b{part}m_{g}"] = full[g], low[g]
    vec = np.stack([vec[n] for n in VECS], 1)

    def v_bias(b):
        m = head_blocks(b.reshape(1, P), (0,)).copy()
        m.reshape(H, 32)[:, 8] = 1.0
        return np.repeat(m, P, 0)

    eye = np.eye(P, dtype=f32)
    avg8 = np.kron(np.eye(H, dtype=f32), np.full((8, 8), 0.125, f32))
    dsel = np.zeros((P, P), f32)
    for j in range(4):
        dsel[32 * j + 8, 32 * j:32 * j + 32] = 1.0
    inv = (f32(1.0) / f32(10000.0) ** (np.arange(0, 64, 2, dtype=f32) / f32(64))).astype(f32)
    ang = (np.arange(N, dtype=f32)[:, None] * inv[None, :]).astype(f32)
    rope_c = np.tile(np.repeat(np.cos(ang).T, 2, 0), (2, 1)).astype(f32)
    sign = np.tile(np.array([-1.0, 1.0], f32), P // 2)[:, None]
    rope_s = (np.tile(np.repeat(np.sin(ang).T, 2, 0), (2, 1)) * sign).astype(f32)
    ca_in, qkv3 = L1["ca_in_w"].T, L3["W_qkv"]
    part3 = [qkv3[:, i * P:(i + 1) * P] for i in range(3)]
    kept = {
        "avg": np.full((P, P), 1.0 / P, f32), "avg8": avg8, "dsel": dsel, "ones": np.ones((P, 64), f32),
        "rope_c": rope_c, "rope_s": rope_s,
        "L0ff1": L0["ff_w1"], "L0ff2": chunks(L0["ff_w2"]),
        "pick_qk": head_blocks(eye, STACK), "pick_v": head_blocks(eye, (0,)), "L1s_wo": out_rows(eye),
        "L1c_q": head_blocks(ca_in[:, 0:P], STACK), "L1c_k": head_blocks(ca_in[:, P:2 * P], STACK),
        "L1c_v": head_blocks(ca_in[:, 2 * P:], (0,)), "L1c_wo": out_rows(L1["ca_out_w"].T),
        "L1w1": L1["w1"].T, "L1w3": L1["w3"].T, "L1w2": chunks(L1["w2"].T), "L1c_bv": v_bias(L1["ca_in_b"][2 * P:]),
        "L2ff1": L2["ff_w1"], "L2ff2": chunks(L2["ff_w2"]),
        "L3s_q": head_blocks(part3[0], STACK), "L3s_k": head_blocks(part3[1], STACK),
        "L3s_v": head_blocks(part3[2], (0,)), "L3s_wo": out_rows(L3["W_proj"]), "L3s_bv": v_bias(L3["b_qkv"][2 * P:]),
        "L3c_q": head_blocks(L3["W_q"], STACK), "L3c_k": head_blocks(L3["W_k"], STACK),
        "L3c_v": head_blocks(L3["W_v"], (0,)), "L3c_wo": out_rows(L3["W_out"]),
        "L3ff1": L3["W_fc1"], "L3ff2": chunks(L3["W_fc2"]),
        "bv_ones": v_bias(np.zeros(P, f32)),
    }
    kept = np.concatenate([kept[n] for n, _ in KEPT], 1)

    def wide_weights(q, k, v, o, swapped):
        parts = [rows128(q), rows128(k), rows128(v), chunks(o)]
        if swapped:
            parts += [rows128(swap_pairs(q)), rows128(swap_pairs(k))]
        return np.concatenate(parts, 1)

    mid = H * 64
    arrays = {
        "x_in": I["x"].reshape(B * N, D).T, "ctx_in": I["ctx_768"].reshape(B * NC, DC).T,
        "cond_in": I["cond_1024"].T, "vec_in": vec, "ident_in": np.eye(P).astype(mybir.dt.np(BF16)),
        "mod_w_in": mod_w, "mod_b_in": mod_b,
        "cond_w_in": np.concatenate([rows128(L1["cond_w"].T), rows128(L3["W_ctx"])], 1),
        "kept_in": kept,
        "self0_in": wide_weights(L0["sa_wq"], L0["sa_wkv"][:, 0:mid], L0["sa_wkv"][:, mid:], L0["sa_wo"], True),
        "cross0_in": wide_weights(L0["ca_wq"], L0["ca_wkv"][:, 0:mid], L0["ca_wkv"][:, mid:], L0["ca_wo"], True),
        "self2_in": wide_weights(L2["q1"], L2["k1"], L2["v1"], L2["o1_w"], False),
        "cross2_in": wide_weights(L2["q2"], L2["k2"], L2["v2"], L2["o2_w"], False),
    }
    arrays = {n: np.ascontiguousarray(a) for n, a in arrays.items()}
    nc = bacc.Bacc("TRN2", target_bir_lowering=False, num_devices=1, dynamic_dma_scratch_size=1024)
    args = [nc.dram_tensor(n, a.shape, mybir.dt.from_np(a.dtype), kind="ExternalInput").ap()
            for n, a in arrays.items()]
    out = nc.dram_tensor("out", (P, B * N), F32, kind="ExternalOutput").ap()
    build(nc, *args, out)
    r = run_bass_kernel_spmd(nc, [arrays], core_ids=[0])
    return r.results[0]["out"].T.reshape(B, N, D)
```

```python
from contextlib import ExitStack

import concourse.bass as bass
import concourse.mybir as mybir
import numpy as np

F32 = mybir.dt.float32
BF16 = mybir.dt.bfloat16
ACT = mybir.ActivationFunctionType
ALU = mybir.AluOpType
AXIS_X = mybir.AxisListType.X

P = 128
B, N, D = 4, 512, 128
NC, DC = 77, 96
H = 16
QT = N // P
FF = 4 * D
FC = FF // P
SLOTS = 2
EXP_LN_SET = 6

MOD_SCALES = ["L0g1", "L0g2", "L1sc_sa", "L1sc_ca", "L1sc_ff", "L2s1", "L2s2", "L2s3",
              "L3sc_msa", "L3sc_x", "L3sc_mlp"]
MOD_REST = ["L0b1", "L0b2", "L1sh_sa", "L1sh_ca", "L1sh_ff", "L2t1", "L2t2", "L2t3",
            "L3sh_msa", "L3sh_x", "L3sh_mlp", "L1ga_sa", "L1ga_ca", "L1ga_ff"]
MOD_DERIVED = ["L0A1", "L0B1", "L0A2", "L0B2", "L1gb_ca"]
MODS = MOD_SCALES + MOD_REST + MOD_DERIVED
NM = len(MOD_SCALES) + len(MOD_REST)
MOD = {n: i for i, n in enumerate(MODS)}
LN_MODS = {(0, 0): ("L0A1", "L0B1"), (0, 1): ("L0A1", "L0B1"), (0, 2): ("L0A2", "L0B2"),
           (1, 0): ("L1sc_sa", "L1sh_sa"), (1, 1): ("L1sc_ca", "L1sh_ca"), (1, 2): ("L1sc_ff", "L1sh_ff"),
           (2, 0): ("L2s1", "L2t1"), (2, 1): ("L2s2", "L2t2"), (2, 2): ("L2s3", "L2t3"),
           (3, 0): ("L3sc_msa", "L3sh_msa"), (3, 1): ("L3sc_x", "L3sh_x"), (3, 2): ("L3sc_mlp", "L3sh_mlp")}
LN_EPS = ["eps5", "eps6", "eps5", "eps6"]

VECS = (["eps5", "eps6", "lw1", "lb1", "lw2", "lb2", "cw", "cb", "L1cond_b", "L3b_ctx", "L1bo_ca",
         "L0bo_sa", "L0bo_ca", "L0ff_b2", "L2bo_sa", "L2bo_ca", "L2ff_b2", "L3bo_sa", "L3bo_ca", "L3ff_b2",
         "qn_w", "qn_b", "kn_w", "kn_b", "qmask", "kmask", "kones"]
        + [f"L0ff_b1_{c}" for c in range(FC)] + [f"L3ff_b1_{c}" for c in range(FC)]
        + [f"L2ff_a_{c}" for c in range(FC)] + [f"L2ff_g_{c}" for c in range(FC)]
        + [f"{a}_b{w}{m}_{g}" for a in ("L1c", "L3s") for w in "qk" for m in ("", "m") for g in range(4)])
VEC = {n: i for i, n in enumerate(VECS)}

KEPT = [("avg", P), ("avg8", P), ("dsel", P), ("ones", 64), ("rope_c", N), ("rope_s", N),
        ("L0ff1", FF), ("L0ff2", FF),
        ("pick_qk", 512), ("pick_v", 512), ("L1s_wo", 512), ("L1c_q", 512), ("L1c_k", 512), ("L1c_v", 512),
        ("L1c_wo", 512), ("L1w1", FF), ("L1w3", FF), ("L1w2", FF), ("L1c_bv", 512),
        ("L2ff1", 2 * FF), ("L2ff2", FF),
        ("L3s_q", 512), ("L3s_k", 512), ("L3s_v", 512), ("L3s_wo", 512), ("L3s_bv", 512),
        ("L3c_q", 512), ("L3c_k", 512), ("L3c_v", 512), ("L3c_wo", 512), ("L3ff1", FF), ("L3ff2", FF),
        ("bv_ones", 512)]
WIDE0 = [("q", 1024), ("k", 1024), ("v", 1024), ("wo", 1024), ("qs", 1024), ("ks", 1024)]


def offsets(pieces):
    at, out = 0, {}
    for name, n in pieces:
        out[name] = (at, n)
        at += n
    return out, at


KEPT_AT, KEPT_N = offsets(KEPT)
FIRST_N = KEPT_AT["L0ff1"][0]
WIDE_AT, WIDE_N = offsets(WIDE0)
WIDE2_N = 4 * 1024


class Attention:

    def __init__(self, layer, cross):
        self.layer, self.cross = layer, cross
        self.wide = layer in (0, 2)
        self.dh = 64 if self.wide else 8
        self.rope = layer == 0
        self.heads = 2 if self.wide else 4
        self.groups = H // self.heads
        self.keys = NC if cross else N
        self.tiles = [NC] if cross else [P] * QT
        self.scale = float(self.dh) ** -0.5
        self.name = f"L{layer}{'c' if cross else 's'}"
        self.vcols = H * (64 if self.wide else 32)


ATTENTIONS = [Attention(layer, cross) for layer in range(4) for cross in (False, True)]


class Group:

    def __init__(self, n, a, s, g):
        self.n, self.a, self.s, self.g = n, a, s, g
        self.region = self.half = self.small = self.before = self.start = self.fresh = self.first_user = None

    def q_tile(self, ring, j, low):
        if not self.a.wide:
            i = 4 * self.half
        elif self.a.cross:
            i = 4 * self.half + 2 * j + low
        else:
            i = 4 * j + low
        return ring[:, self.region, i, :]

    def k_tile(self, ring, small, j, low):
        if self.a.cross:
            if self.a.wide:
                return small[:, self.small, 2 * j + low, :]
            return ring[:, self.region, 4 * self.half + 1, j * NC:(j + 1) * NC]
        return ring[:, self.region, 4 * j + 2 + low if self.a.wide else 1 + j, :]


def make_groups():
    groups, region, half, start = [], 0, 0, 0
    for a in ATTENTIONS:
        for s in range(SLOTS):
            for g in range(a.groups):
                new = Group(len(groups), a, s, g)
                new.region, new.half, new.start = region, half, start
                new.small = (s * a.groups + g) % 6
                turn = s * a.groups + g
                new.fresh = turn < 3 if not a.cross else (not a.wide and turn < 6)
                for old in reversed(groups):
                    if old.region == region and not (a.cross and old.a.cross and old.half != half):
                        new.before = old
                        break
                groups.append(new)
                start += a.heads * len(a.tiles)
                if a.cross and half == 0:
                    half = 1
                else:
                    region, half = (region + 1) % 3, 0
    return groups


class Step:

    def __init__(self, kind, a=None, s=None, G=None, j=None, t=None, c=None, ln=None, head_norm=False, layer=None,
                 part=None):
        self.kind, self.layer, self.G, self.j, self.t, self.c = kind, layer, G, j, t, c
        self.a, self.s = (G.a, G.s) if G is not None else (a, s)
        self.ln, self.head_norm, self.part = ln, head_norm, part


def dense_before(a, s):
    steps = [Step("mean", s=s, ln=(a.layer, int(a.cross))), Step("var", s=s, ln=(a.layer, int(a.cross)))]
    if a.layer == 1 and not a.cross:
        steps += [Step("mean", s=s, ln=(1, "qk"), head_norm=True), Step("var", s=s, ln=(1, "qk"), head_norm=True)]
    return steps + [Step("v", s=s, a=a, t=t, c=c) for t in range(len(a.tiles)) for c in range(a.vcols // 512)]


def feed_forward(layer, s):
    return ([Step("mean", s=s, ln=(layer, 2)), Step("var", s=s, ln=(layer, 2))]
            + [Step("up", s=s, layer=layer, c=c) for c in range(FC)] + [Step("down", s=s, layer=layer)])


def make_plan():
    groups = make_groups()
    ends = {G.n: G.start + G.a.heads * len(G.a.tiles) for G in groups}
    timed = []

    def put(time, order, step):
        timed.append((time, order, len(timed), step))

    project_at = {}
    for G in groups:
        a = G.a
        lead = {(True, False): 11, (True, True): 5, (False, False): 20, (False, True): 8}[a.wide, a.cross]
        first = G.start - lead
        at = first - 5
        if G.before is not None:
            at = max(at, ends[G.before.n])
        project_at[G.n] = at
        put(at, 4, Step("project", G=G, part="q"))
        put(at + 1, 4, Step("project", G=G, part="k"))
        nmax = 1 if a.cross else QT
        k = max(first, at + 2)
        for j in range(a.heads):
            for t in range(nmax):
                put(k, 1, Step("max", G=G, j=j, t=t))
                k += 1
            put(k - 1, 2, Step("shift", G=G, j=j))
        put(min(k, max(G.start - 1, k - 1)), 3, Step("rows", G=G))
        k = G.start
        for t in range(len(a.tiles)):
            for j in range(a.heads):
                put(k, 0 if G.n or k else 3.5, Step("scores", G=G, j=j, t=t))
                if j % 2:
                    put(k + 2, 2.5, Step("values", G=G, j=j - 1, t=t))
                k += 1
        put(k + 1 if a.wide else k + 2, 2.7, Step("norm", G=G))
        put(k + 3, 3, Step("out", G=G))

    for n, a in enumerate(ATTENTIONS):
        for s in range(SLOTS):
            steps = dense_before(a, s)
            own = [G for G in groups if G.a is a and G.s == s]
            if n:
                last = [G for G in groups if G.a is ATTENTIONS[n - 1] and G.s == s][-1]
                begin = ends[last.n] + 4
                if not a.cross:
                    steps = feed_forward(a.layer - 1, s) + steps
            elif s == 0:
                begin = -1000
            else:
                begin = 0
            end = project_at[own[0].n]
            spread(put, steps, begin, end)
    for s in range(SLOTS):
        last = [G for G in groups if G.a is ATTENTIONS[-1] and G.s == s][-1]
        spread(put, feed_forward(3, s), ends[last.n] + 4, ends[last.n] + 20)
    timed.sort(key=lambda x: x[:3])
    return in_order([st for _, _, _, st in timed])


def spread(put, steps, begin, end):
    ups = [n for n, st in enumerate(steps) if st.kind == "up"]
    span = max(end - begin, 1)
    for n, st in enumerate(steps):
        place = ups[0] if n in ups else n
        put(begin + int(span * place / len(steps)), 5, st)


def in_order(steps):
    done, out, waiting = set(), [], []

    def needs(st):
        if st.kind in ("mean", "project", "v"):
            a, s = st.a, st.s
            if st.kind == "project":
                return [("v", s, a.name)]
            if st.kind == "mean" and not st.head_norm:
                layer, stage = st.ln
                if stage == 0:
                    return [("down", layer - 1, s)] if layer else []
                return [("outs", s, f"L{layer}{'sc'[stage - 1]}")]
        if st.kind == "max":
            return [("project", st.G.n)]
        if st.kind == "shift":
            return [("max", st.G.n, st.j)]
        if st.kind == "rows":
            return [("shifts", st.G.n)]
        if st.kind == "scores":
            return [("rows", st.G.n)]
        if st.kind == "values":
            return [("scores", st.G.n, st.j + 1, st.t), ("v", st.s, st.a.name)]
        if st.kind == "norm":
            return [("values", st.G.n)]
        if st.kind == "out":
            return [("norm", st.G.n)]
        return []

    def gives(st):
        if st.kind == "v" and st.t == len(st.a.tiles) - 1 and st.c == st.a.vcols // 512 - 1:
            return ("v", st.s, st.a.name)
        if st.kind == "down":
            return ("down", st.layer, st.s)
        if st.kind == "out" and st.G.g == st.a.groups - 1:
            return ("outs", st.s, st.a.name)
        if st.kind == "project" and st.part == "k":
            return ("project", st.G.n)
        if st.kind == "max" and st.t == (0 if st.a.cross else QT - 1):
            return ("max", st.G.n, st.j)
        if st.kind == "shift" and st.j == st.a.heads - 1:
            return ("shifts", st.G.n)
        if st.kind == "rows":
            return ("rows", st.G.n)
        if st.kind == "scores":
            return ("scores", st.G.n, st.j, st.t)
        if st.kind == "values" and st.t == len(st.a.tiles) - 1 and st.j == st.a.heads - 2:
            return ("values", st.G.n)
        if st.kind == "norm":
            return ("norm", st.G.n)
        return None

    def lane(st):
        if st.kind in ("mean", "var", "up", "down", "v"):
            return "dense"
        return st.kind

    for st in steps:
        waiting.append(st)
        again = True
        while again:
            again, blocked, left = False, set(), []
            for x in waiting:
                if lane(x) in blocked or any(n not in done for n in needs(x)):
                    blocked.add(lane(x))
                    left.append(x)
                else:
                    out.append(x)
                    if gives(x) is not None:
                        done.add(gives(x))
                    again = True
            waiting = left
    assert not waiting
    return out


def number(plan):
    at, bank, kinds = {}, 0, {}
    for st in plan:
        a, G, kind = st.a, st.G, st.kind
        st.bank = bank
        if kind == "var":
            st.n = kinds["mean"] - 1
            at["ln", st.s, st.ln] = st.n
        else:
            st.n = kinds.get(kind, 0)
            kinds[kind] = st.n + 1
        if kind in ("mean", "var", "v", "rows", "out", "down"):
            bank += 1
        if kind == "up":
            bank += 2 if st.layer in (1, 2) else 1
        if kind == "project":
            bank += 2 if a.rope else 1
            st.clears = a.wide and st.part == "q"
            st.sets = G.fresh and st.part == "k"
            if st.clears or st.sets:
                kinds["prepared"] = kinds.get("prepared", 0) + 1
            st.prepared = kinds.get("prepared", 0)
            if a.rope:
                st.rope = kinds["rope"] = kinds.get("rope", -1) + 1
            at["project", G.n, st.part] = st
        if kind == "v":
            at["v", st.s, a.name] = st.bank
        if kind == "up":
            at["up"] = bank - 1
        if kind == "down":
            st.up = at["up"]
        if kind == "rows":
            at["rows", G.n] = st.bank
        if kind == "shift":
            at["shift", G.n, st.j] = st.n
            at["shift_n", st.n] = G
        if kind == "max":
            at["max", G.n, st.j] = st.n
        if kind == "scores":
            at["scores", G.n, st.j, st.t] = st.n
            at["scores_end", G.n] = st.n + 1
        if kind == "values":
            at["values", G.n] = st.n
        if kind == "norm":
            at["norm", G.n] = st.n
            at["norm_n", st.n] = st
            if not a.wide:
                st.narrow = kinds["narrow"] = kinds.get("narrow", -1) + 1
        assert kind != "scores" or st.n < 4 or kinds["values"] >= st.n // 2 - 1
        assert kind != "shift" or st.n < 8 or ("rows", at["shift_n", st.n - 8].n) in at
        if kind in ("mean", "out", "down"):
            st.x = at.get(("x", st.s))
        if kind in ("out", "down"):
            at["x", st.s] = st.bank
            if kind == "out":
                at["out", G.n] = st.bank
            else:
                at["down", st.layer, st.s] = st.bank
    return at


def build(nc, x_in, ctx_in, cond_in, vec_in, ident_in, mod_w_in, mod_b_in, cond_w_in, kept_in,
          self0_in, cross0_in, self2_in, cross2_in, out):
    plan = make_plan()
    at = number(plan)
    with ExitStack() as ctx:
        def sb(name, shape, dt=F32):
            return ctx.enter_context(nc.sbuf_tensor(name, shape, dt))

        def sem(name):
            return ctx.enter_context(nc.semaphore(name))

        kept = sb("kept", [P, KEPT_N])
        wide_self, wide_cross = sb("wide_self", [P, WIDE_N]), sb("wide_cross", [P, WIDE_N])
        vec, mod_b = sb("vec", [P, len(VECS)]), sb("mod_b", [P, NM])
        ident = sb("ident", [P, P], BF16)
        mods, cur = sb("mods", [P, len(MODS), B]), sb("cur", [P, len(MODS), SLOTS])
        cond, silu = sb("cond", [P, B]), sb("silu", [P, B])
        ctx_all, ctx_cur = sb("ctx_all", [P, 4, B * NC]), sb("ctx_cur", [P, 4, SLOTS * NC])
        xs, hs = sb("xs", [P, SLOTS, N]), sb("hs", [P, SLOTS, N])
        centred, rstd = sb("centred", [P, N]), sb("rstd", [P, N])
        squared = rstd
        vs = sb("vs", [P, SLOTS, QT, 1024])
        ring = sb("ring", [P, 3, 8, N], BF16)
        small = sb("small", [P, 6, 4, NC], BF16)
        his, los = sb("his", [P, 2, N], BF16), sb("los", [P, 2, N], BF16)
        shift_parts = sb("shift_parts", [P, 8, QT, 32], BF16)
        neg_max = sb("neg_max", [P, 8, QT])
        probs = sb("probs", [P, 4, N])
        heads_out, recip, unnormed = sb("heads_out", [P, 2, N]), sb("recip", [P, N]), sb("unnormed", [P, N])
        rope_a, rope_b = unnormed, sb("rope_b", [P, N])
        hidden = sb("hidden", [P, FC, N])

        general = [ctx.enter_context(nc.psum_tensor(f"general{i}", [P, N], F32)) for i in range(2)]
        max_bank = [ctx.enter_context(nc.psum_tensor(f"max_bank{i}", [P, N], F32)) for i in range(2)]
        score_bank = [ctx.enter_context(nc.psum_tensor(f"score_bank{i}", [P, N], F32)) for i in range(2)]
        value_bank = ctx.enter_context(nc.psum_tensor("value_bank", [P, N], F32))
        denom_bank = ctx.enter_context(nc.psum_tensor("denom_bank", [P, N], F32))

        def w(name, lo=0, n=None):
            first, width = KEPT_AT[name]
            return kept[:, first + lo:first + lo + (width if n is None else n)]

        def wide(a, name, lo, n):
            first = WIDE_AT[name][0] + lo
            return (wide_cross if a.cross else wide_self)[:, first:first + n]

        def v_col(name):
            return vec[:, VEC[name]:VEC[name] + 1]

        def mod(name, s):
            return cur[:, MOD[name], s:s + 1]

        def load_exp_ln():
            nc.scalar.add_instruction(mybir.InstLoadActFuncSet(
                act_func_set_id=EXP_LN_SET, name=nc.get_next_instruction_name(),
                engine=mybir.EngineType.Activation))

        const_loaded, first_loaded, rest_loaded = sem("const_loaded"), sem("first_loaded"), sem("rest_loaded")
        self0_loaded, cross0_loaded = sem("self0_loaded"), sem("cross0_loaded")
        setup_vector, setup_scalar, setup_tensor, setup_pool = (
            sem("setup_vector"), sem("setup_scalar"), sem("setup_tensor"), sem("setup_pool"))

        staging = ring[:, :, :, :].rearrange("p r k n -> p (r k n)").bitcast(F32)
        mod_w = staging[:, 0:NM * P]
        cond_w = staging[:, NM * P:(NM + 2) * P]
        NK4 = B * NC

        with nc.Block() as block:
            @block.sync
            def _(sp):
                sp.dma_start(cond[:], cond_in).then_inc(const_loaded, 16)
                sp.dma_start(vec[:], vec_in).then_inc(const_loaded, 16)
                sp.dma_start(mod_b[:], mod_b_in).then_inc(const_loaded, 16)
                sp.dma_start(mod_w, mod_w_in).then_inc(const_loaded, 16)
                sp.dma_start(cond_w, cond_w_in).then_inc(const_loaded, 16)
                sp.dma_start(ident[:], ident_in).then_inc(const_loaded, 16)
                sp.wait_ge(setup_vector, 1)
                sp.dma_start(ctx_all[0:DC, 0, :], ctx_in).then_inc(const_loaded, 16)
                sp.dma_start(ctx_all[0:DC, 1, :], ctx_in).then_inc(const_loaded, 16)
                sp.dma_start(kept[:, 0:FIRST_N], kept_in[:, 0:FIRST_N]).then_inc(first_loaded, 16)
                sp.dma_start(wide_self[:], self0_in).then_inc(self0_loaded, 16)
                sp.dma_start(wide_cross[:], cross0_in).then_inc(cross0_loaded, 16)
                sp.dma_start(kept[:, FIRST_N:KEPT_N], kept_in[:, FIRST_N:KEPT_N]).then_inc(rest_loaded, 16)
                sp.wait_ge(const_loaded, 8 * 16)
                sp.wait_ge(first_loaded, 16)

            @block.gpsimd
            def _(pool):
                nc.gpsimd.memset(shift_parts[:], 0.0).then_inc(setup_pool, 1)
                nc.gpsimd.memset(recip[:], 1.0 / DC).then_inc(setup_pool, 1)
                pool.wait_ge(setup_pool, 2)
                nc.gpsimd.memset(small[64:128, :, :, :], 0.0).then_inc(setup_pool, 1)
                pool.wait_ge(setup_pool, 3)
                nc.gpsimd.memset(small[64:66, :, 1, :], 1.0).then_inc(setup_pool, 1)
                nc.gpsimd.memset(small[96:98, :, 3, :], 1.0).then_inc(setup_pool, 1)
                pool.wait_ge(setup_pool, 5)

            @block.vector
            def _(dve):
                nc.vector.memset(ctx_all[:], 0.0).then_inc(setup_vector, 1)
                dve.wait_ge(setup_scalar, 1)
                nc.vector.tensor_scalar(silu[:], silu[:], 1.0, None, ALU.add).then_inc(setup_vector, 1)
                dve.wait_ge(setup_vector, 2)
                nc.vector.reciprocal(silu[:], silu[:]).then_inc(setup_vector, 1)
                dve.wait_ge(setup_vector, 3)
                nc.vector.tensor_tensor(silu[:], silu[:], cond[:], ALU.mult).then_inc(setup_vector, 1)
                dve.wait_ge(setup_tensor, 1)
                raw = general[0][:, 0:NM * B].rearrange("p (m b) -> p m b", b=B)
                nc.vector.tensor_tensor(mods[:, 0:NM, :], raw, mod_b[:].unsqueeze(2).broadcast_to([P, NM, B]),
                                        ALU.add).then_inc(setup_vector, 1)
                dve.wait_ge(setup_vector, 5)
                ns = len(MOD_SCALES)
                nc.vector.tensor_scalar(mods[:, 0:ns, :], mods[:, 0:ns, :], 1.0, None,
                                        ALU.add).then_inc(setup_vector, 1)
                dve.wait_ge(setup_vector, 6)
                for i, (g, b, lw, lb) in enumerate((("L0g1", "L0b1", "lw1", "lb1"), ("L0g2", "L0b2", "lw2", "lb2"))):
                    nc.vector.tensor_scalar(mods[:, MOD[f"L0A{i + 1}"], :], mods[:, MOD[g], :], v_col(lw), None,
                                            ALU.mult).then_inc(setup_vector, 1)
                    nc.vector.scalar_tensor_tensor(mods[:, MOD[f"L0B{i + 1}"], :], mods[:, MOD[g], :], v_col(lb),
                                                   mods[:, MOD[b], :], ALU.mult, ALU.add).then_inc(setup_vector, 1)
                nc.vector.tensor_scalar(mods[:, MOD["L1gb_ca"], :], mods[:, MOD["L1ga_ca"], :], v_col("L1bo_ca"),
                                        None, ALU.mult).then_inc(setup_vector, 1)
                dve.wait_ge(setup_tensor, 2)
                nc.vector.tensor_tensor(hidden[:, 0, 0:NK4], ctx_all[:, 0, :], general[1][:, 0:NK4],
                                        ALU.subtract).then_inc(setup_vector, 1)
                dve.wait_ge(setup_scalar, 4)
                nc.vector.tensor_tensor(hidden[:, 2, 0:NK4], hidden[:, 0, 0:NK4], hidden[:, 3, 0:NK4],
                                        ALU.mult).then_inc(setup_vector, 1)
                dve.wait_ge(setup_vector, 13)
                nc.vector.tensor_scalar(ctx_all[:, 0, :], hidden[:, 2, 0:NK4], v_col("cw"), v_col("cb"),
                                        ALU.mult, ALU.add).then_inc(setup_vector, 1)
                dve.wait_ge(setup_vector, 14)

            @block.scalar
            def _(act):
                load_exp_ln()
                act.wait_ge(const_loaded, 8 * 16)
                nc.scalar.activation(silu[:], cond[:], ACT.Exp, scale=-1.0).then_inc(setup_scalar, 1)
                act.wait_ge(setup_vector, 12)
                nc.scalar.activation(hidden[:, 1, 0:NK4], hidden[:, 0, 0:NK4], ACT.Square).then_inc(setup_scalar, 1)
                act.wait_ge(setup_tensor, 3)
                nc.scalar.activation(hidden[:, 2, 0:NK4], general[1][:, 0:NK4], ACT.Ln,
                                     bias=v_col("eps5")).then_inc(setup_scalar, 1)
                act.wait_ge(setup_scalar, 3)
                nc.scalar.activation(hidden[:, 3, 0:NK4], hidden[:, 2, 0:NK4], ACT.Exp, scale=-0.5)\
                    .then_inc(setup_scalar, 1)
                act.wait_ge(setup_tensor, 4)
                nc.scalar.activation(ctx_all[:, 2, :], max_bank[0][:, 0:NK4], ACT.Identity,
                                     bias=v_col("L1cond_b")).then_inc(setup_scalar, 1)
                nc.scalar.activation(ctx_all[:, 3, :], max_bank[1][:, 0:NK4], ACT.Identity,
                                     bias=v_col("L3b_ctx")).then_inc(setup_scalar, 1)
                act.wait_ge(setup_scalar, 6)

            @block.tensor
            def _(pe):
                pe.wait_ge(const_loaded, 8 * 16)
                pe.wait_ge(setup_vector, 4)
                for i, name in enumerate(MOD_SCALES + MOD_REST):
                    moving = silu if name[:2] in ("L1", "L3") else cond
                    last = nc.tensor.matmul(general[0][:, i * B:(i + 1) * B], mod_w[:, i * P:(i + 1) * P],
                                            moving[:], start=True, stop=True)
                last.then_inc(setup_tensor, 1)
                pe.wait_ge(setup_pool, 2)
                nc.tensor.matmul(general[1][:, 0:NK4], recip[:, 0:P], ctx_all[:, 0, :], start=True,
                                 stop=True).then_inc(setup_tensor, 1)
                pe.wait_ge(setup_scalar, 2)
                nc.tensor.matmul(general[1][:, 0:NK4], recip[0:DC, 0:P], hidden[0:DC, 1, 0:NK4], start=True,
                                 stop=True).then_inc(setup_tensor, 1)
                for i in range(2):
                    last = nc.tensor.matmul(max_bank[i][:, 0:NK4], cond_w[:, i * P:(i + 1) * P],
                                            ctx_all[:, 1, :], start=True, stop=True)
                last.then_inc(setup_tensor, 1)

        names = ("bank_filled bank_done0 bank_done1 max_filled max_reduced shift_split scores_filled probs_ready "
                 "values_done hi_ready split_done rope_sum operands_set unnormed_ready "
                 "denom_filled recip_ready heads_ready squares_ready rstd_ready normed_ready h_ready qk_ready "
                 "vector_chain scalar_chain pool_chain slots_ready x_loaded self2_loaded cross2_loaded reloaded stored").split()
        sems = {n: sem(n) for n in names}
        bank_filled, max_filled, max_reduced = sems["bank_filled"], sems["max_filled"], sems["max_reduced"]
        bank_done = [sems["bank_done0"], sems["bank_done1"]]
        shift_split, scores_filled, probs_ready = sems["shift_split"], sems["scores_filled"], sems["probs_ready"]
        values_done, hi_ready, split_done = sems["values_done"], sems["hi_ready"], sems["split_done"]
        rope_sum, operands_set = sems["rope_sum"], sems["operands_set"]
        unnormed_ready, denom_filled = sems["unnormed_ready"], sems["denom_filled"]
        recip_ready, heads_ready, squares_ready = sems["recip_ready"], sems["heads_ready"], sems["squares_ready"]
        rstd_ready, normed_ready, h_ready = sems["rstd_ready"], sems["normed_ready"], sems["h_ready"]
        vector_chain, scalar_chain, pool_chain = sems["vector_chain"], sems["scalar_chain"], sems["pool_chain"]
        slots_ready, x_loaded = sems["slots_ready"], sems["x_loaded"]
        self2_loaded, cross2_loaded = sems["self2_loaded"], sems["cross2_loaded"]
        reloaded, stored = sems["reloaded"], sems["stored"]

        def bank_at(i):
            return general[i % 2]

        def wait_bank_free(eng, i):
            if i >= 2:
                eng.wait_ge(bank_done[i % 2], i // 2)

        def wait_bank_done(eng, i):
            eng.wait_ge(bank_done[i % 2], i // 2 + 1)

        def wait_x(eng, st):
            if st.x is None:
                eng.wait_ge(x_loaded, 16 * SLOTS)
            else:
                wait_bank_done(eng, st.x)

        def source(a, s, w_):
            if w_ == "k" and a.cross:
                kind = {0: 0, 2: 1, 1: 2, 3: 3}[a.layer]
                return ctx_cur[:, kind, s * NC:(s + 1) * NC]
            if a.layer == 1 and not a.cross:
                return vs[:, s, 0 if w_ == "q" else 1, 512:1024]
            return hs[:, s, :]

        def wait_source(eng, a, s):
            eng.wait_ge(h_ready, at["ln", s, (a.layer, int(a.cross))] + 1)
            if a.layer == 1 and not a.cross:
                eng.wait_ge(h_ready, at["ln", s, (1, "qk")] + 1)

        def wait_weights(eng, a):
            if a.wide:
                eng.wait_ge({"L0s": self0_loaded, "L0c": cross0_loaded, "L2s": self2_loaded,
                             "L2c": cross2_loaded}[a.name], 16)

        def wait_ring_free(eng, G):
            if G.before is not None:
                eng.wait_ge(scores_filled, at["scores_end", G.before.n])

        def has_bias(a):
            return a.name in ("L1c", "L3s")

        def last_out(n):
            return max(at["out", G.n] for G in (st.G for st in plan if st.kind == "out") if G.a is ATTENTIONS[n])

        def wait_output_banks_free(pe, a, n):
            if n:
                old = at["norm_n", n - 1]
                if old.a.wide or a.wide:
                    pe.wait_ge(heads_ready, n)
                else:
                    pe.wait_ge(unnormed_ready, old.narrow + 1)

        def up_weights(st):
            if st.layer == 1:
                return [w("L1w1", st.c * P, P), w("L1w3", st.c * P, P)]
            if st.layer == 2:
                return [w("L2ff1", FF + st.c * P, P), w("L2ff1", st.c * P, P)]
            return [w(f"L{st.layer}ff1", st.c * P, P)]


        with nc.Fori(0, B // SLOTS) as pair:
            with nc.Block() as block:
                @block.sync
                def _(sp):
                    for s in range(SLOTS):
                        sp.dma_start(xs[:, s, :], x_in[:, bass.ds((pair * SLOTS + s) * N, N)]).then_inc(x_loaded, 16)
                    for n, tile, src, landed in ((0, wide_self[:, 0:WIDE2_N], self2_in, self2_loaded),
                                                 (1, wide_cross[:, 0:WIDE2_N], cross2_in, cross2_loaded),
                                                 (4, wide_self[:], self0_in, reloaded),
                                                 (5, wide_cross[:], cross0_in, reloaded)):
                        wait_bank_done(sp, last_out(n))
                        sp.dma_start(tile, src).then_inc(landed, 16)
                    for s in range(SLOTS):
                        wait_bank_done(sp, at["down", 3, s])
                        sp.dma_start(out[:, bass.ds((pair * SLOTS + s) * N, N)], xs[:, s, :]).then_inc(stored, 16)
                    sp.wait_ge(stored, 16 * SLOTS)
                    sp.wait_ge(reloaded, 2 * 16)

                @block.tensor
                def _(pe):
                    pe.wait_ge(slots_ready, 2)
                    for st in plan:
                        a = st.a
                        i = st.bank
                        if st.kind == "mean":
                            if st.head_norm:
                                pe.wait_ge(h_ready, at["ln", st.s, (1, 0)] + 1)
                            else:
                                wait_x(pe, st)
                            wait_bank_free(pe, i)
                            src = hs[:, st.s, :] if st.head_norm else xs[:, st.s, :]
                            nc.tensor.matmul(bank_at(i)[:], w("avg8" if st.head_norm else "avg"), src,
                                             start=True, stop=True).then_inc(bank_filled, 1)
                        elif st.kind == "var":
                            pe.wait_ge(squares_ready, st.n + 1)
                            wait_bank_free(pe, i)
                            nc.tensor.matmul(bank_at(i)[:], w("avg8" if st.head_norm else "avg"), squared[:],
                                             start=True, stop=True).then_inc(bank_filled, 1)
                        elif st.kind == "v":
                            pe.wait_ge(h_ready, at["ln", st.s, (a.layer, int(a.cross))] + 1)
                            wait_weights(pe, a)
                            wait_bank_free(pe, i)
                            n = a.tiles[st.t]
                            src = source(a, st.s, "k") if a.cross else hs[:, st.s, st.t * P:(st.t + 1) * P]
                            if a.wide:
                                right = wide(a, "v", st.c * 512, 512)
                            else:
                                right = w("pick_v" if a.name == "L1s" else a.name + "_v")
                            nc.tensor.matmul(bank_at(i)[0:n, :], src, right, start=True, stop=True)\
                                .then_inc(bank_filled, 1)
                        elif st.kind == "project":
                            wait_source(pe, a, st.s)
                            wait_weights(pe, a)
                            src = source(a, st.s, st.part)
                            n = src.shape[-1]
                            for swapped in range(1 + a.rope):
                                if a.wide:
                                    left = wide(a, st.part + "s" * swapped, st.G.g * P, P)
                                elif a.name == "L1s":
                                    left = w("pick_qk", st.G.g * P, P)
                                else:
                                    left = w(f"{a.name}_{st.part}", st.G.g * P, P)
                                wait_bank_free(pe, i)
                                nc.tensor.matmul(bank_at(i)[:, 0:n], left, src, start=True, stop=True)\
                                    .then_inc(bank_filled, 1)
                                i += 1
                        elif st.kind == "max":
                            G, j = st.G, st.j
                            if j == 0 and st.t == 0:
                                keys = at["project", G.n, "k"]
                                pe.wait_ge(split_done, keys.n + 1)
                                if keys.prepared:
                                    pe.wait_ge(operands_set, keys.prepared)
                            if st.n >= 2:
                                pe.wait_ge(max_reduced, st.n - 1)
                            bank, nk = max_bank[st.n % 2], a.keys
                            q1, k1 = G.q_tile(ring, j, 0), G.k_tile(ring, small, j, 0)
                            q2, k2 = G.q_tile(ring, j, 1), G.k_tile(ring, small, j, 1)
                            for q in (range(QT) if a.cross else (st.t,)):
                                to = bank[:, q * nk:(q + 1) * nk] if a.cross else bank[:]
                                lo, hi = q * P, (q + 1) * P
                                last = nc.tensor.matmul(to, q1[:, lo:hi], k1[:, 0:nk], start=True, stop=not a.wide)
                                if a.wide:
                                    last = nc.tensor.matmul(to, q2[:, lo:hi], k2[:, 0:nk], start=False, stop=True)
                            last.then_inc(max_filled, 1)
                        elif st.kind == "rows":
                            pe.wait_ge(shift_split, at["shift", st.G.n, a.heads - 1] + 1)
                            wait_bank_free(pe, i)
                            for j in range(a.heads):
                                m = at["shift", st.G.n, j] % 8
                                row = 32 * j + (64 if a.wide else 0)
                                for q in range(QT):
                                    last = nc.tensor.matmul(bank_at(i)[row:row + 32, q * P:(q + 1) * P],
                                                            shift_parts[:, m, q, :], ident[:], start=True, stop=True)
                            last.then_inc(bank_filled, 1)
                        elif st.kind == "scores":
                            G, j = st.G, st.j
                            if st.t == 0 and j == 0:
                                wait_bank_done(pe, at["rows", G.n])
                            if st.n >= 2:
                                pe.wait_ge(probs_ready, st.n - 1)
                            bank, nk, lo = score_bank[st.n % 2], a.tiles[st.t], st.t * P
                            last = nc.tensor.matmul(bank[0:nk, :], G.k_tile(ring, small, j, 0)[:, lo:lo + nk],
                                                    G.q_tile(ring, j, 0), start=True, stop=not a.wide)
                            if a.wide:
                                last = nc.tensor.matmul(bank[0:nk, :], G.k_tile(ring, small, j, 1)[:, lo:lo + nk],
                                                        G.q_tile(ring, j, 1), start=False, stop=True)
                            last.then_inc(scores_filled, 1)
                        elif st.kind == "values":
                            n, nk = at["scores", st.G.n, st.j, st.t], a.tiles[st.t]
                            first, last_tile = st.t == 0, st.t == len(a.tiles) - 1
                            if first and st.j == 0:
                                if st.G.g == 0:
                                    wait_bank_done(pe, at["v", st.s, a.name])
                                wait_output_banks_free(pe, a, at["norm", st.G.n])
                            pe.wait_ge(probs_ready, n + 2)
                            pair_of = [(j, a.heads * st.G.g + j, probs[0:nk, (n + j - st.j) % 4, :])
                                       for j in (st.j, st.j + 1)]
                            width = 64 if a.wide else 32
                            for j, h, prob in pair_of:
                                last = nc.tensor.matmul(value_bank[width * j:width * (j + 1), :],
                                                        vs[0:nk, st.s, st.t, h * width:(h + 1) * width], prob,
                                                        start=first, stop=last_tile)
                            if a.wide:
                                for j, h, prob in pair_of:
                                    last = nc.tensor.matmul(denom_bank[64 * j:64 * j + 64, :], w("ones")[0:nk, :],
                                                            prob, start=first, stop=last_tile)
                            last.then_inc(values_done, 1)
                        elif st.kind == "norm" and not a.wide:
                            pe.wait_ge(unnormed_ready, st.narrow + 1)
                            if st.n >= 1:
                                pe.wait_ge(recip_ready, st.n)
                            nc.tensor.matmul(denom_bank[:], w("dsel"), unnormed[:], start=True, stop=True)\
                                .then_inc(denom_filled, 1)
                        elif st.kind == "out":
                            norm = at["norm", st.G.n]
                            pe.wait_ge(heads_ready, norm + 1)
                            wait_bank_free(pe, i)
                            g = st.G.g
                            left = wide(a, "wo", g * P, P) if a.wide else w(a.name + "_wo", g * P, P)
                            nc.tensor.matmul(bank_at(i)[:], left, heads_out[:, norm % 2, :],
                                             start=True, stop=True).then_inc(bank_filled, 1)
                        elif st.kind == "up":
                            pe.wait_ge(h_ready, at["ln", st.s, (st.layer, 2)] + 1)
                            pe.wait_ge(rest_loaded, 16)
                            for left in up_weights(st):
                                wait_bank_free(pe, i)
                                nc.tensor.matmul(bank_at(i)[:], left, hs[:, st.s, :], start=True, stop=True)\
                                    .then_inc(bank_filled, 1)
                                i += 1
                        elif st.kind == "down":
                            wait_bank_free(pe, i)
                            wait_bank_done(pe, st.up)
                            name = {0: "L0ff2", 1: "L1w2", 2: "L2ff2", 3: "L3ff2"}[st.layer]
                            for c in range(FC):
                                last = nc.tensor.matmul(bank_at(i)[:], w(name, c * P, P), hidden[:, c, :],
                                                        start=c == 0, stop=c == FC - 1)
                            last.then_inc(bank_filled, 1)

                @block.scalar
                def _(act):
                    chain = [0]

                    def link(ins):
                        chain[0] += 1
                        ins.then_inc(scalar_chain, 1)
                        act.wait_ge(scalar_chain, chain[0])

                    load_exp_ln()
                    act.wait_ge(slots_ready, 2)
                    for st in plan:
                        a = st.a
                        i = st.bank
                        if st.kind == "mean":
                            wait_bank_done(act, i)
                            if st.n >= 1:
                                act.wait_ge(normed_ready, st.n)
                            nc.scalar.activation(squared[:], centred[:], ACT.Square).then_inc(squares_ready, 1)
                        elif st.kind == "var":
                            act.wait_ge(bank_filled, i + 1)
                            if st.n >= 1:
                                act.wait_ge(normed_ready, st.n)
                            eps = "eps6" if st.head_norm else LN_EPS[st.ln[0]]
                            nc.scalar.activation(rstd[:], bank_at(i)[:], ACT.Ln, bias=v_col(eps))\
                                .then_inc(bank_done[i % 2], 1)
                            wait_bank_done(act, i)
                            nc.scalar.activation(rstd[:], rstd[:], ACT.Exp, scale=-0.5).then_inc(rstd_ready, 1)
                            act.wait_ge(normed_ready, st.n + 1)
                            if st.head_norm:
                                nc.scalar.activation(vs[:, st.s, 0, 512:1024], centred[:], ACT.Identity,
                                                     scale=v_col("qn_w"), bias=v_col("qn_b"))
                                nc.scalar.activation(vs[:, st.s, 1, 512:1024], centred[:], ACT.Identity,
                                                     scale=v_col("kn_w"), bias=v_col("kn_b")).then_inc(h_ready, 1)
                            else:
                                scale, shift = LN_MODS[st.ln]
                                nc.scalar.activation(hs[:, st.s, :], centred[:], ACT.Identity,
                                                     scale=mod(scale, st.s), bias=mod(shift, st.s))\
                                    .then_inc(h_ready, 1)
                        elif st.kind == "v" and a.wide:
                            act.wait_ge(bank_filled, i + 1)
                            n = a.tiles[st.t]
                            nc.scalar.activation(vs[0:n, st.s, st.t, st.c * 512:(st.c + 1) * 512],
                                                 bank_at(i)[0:n, :], ACT.Identity).then_inc(bank_done[i % 2], 1)
                        elif st.kind == "project":
                            n, part = (a.keys if st.part == "k" else N), st.part
                            hi = his[:, st.n % 2, 0:n]
                            if st.n >= 2:
                                act.wait_ge(split_done, st.n - 1)
                            if a.rope:
                                act.wait_ge(rope_sum, st.rope + 1)
                                nc.scalar.activation(hi, rope_a[:, 0:n], ACT.Identity).then_inc(hi_ready, 1)
                                continue
                            act.wait_ge(bank_filled, i + 1)
                            if a.wide:
                                nc.scalar.activation(hi, bank_at(i)[:, 0:n], ACT.Identity).then_inc(hi_ready, 1)
                            else:
                                bias = v_col(f"{a.name}_b{part}m_{st.G.g}") if has_bias(a) else 0.0
                                nc.scalar.activation(hi, bank_at(i)[:, 0:n], ACT.Identity,
                                                     scale=v_col(part + "mask"), bias=bias).then_inc(hi_ready, 1)
                        elif st.kind == "rows" and a.wide:
                            act.wait_ge(bank_filled, i + 1)
                            for j in range(2):
                                last = nc.scalar.activation(st.G.q_tile(ring, j, 1)[64:128, :],
                                                            bank_at(i)[64:128, :], ACT.Identity)
                            last.then_inc(bank_done[i % 2], 1)
                        elif st.kind == "scores":
                            nk = a.tiles[st.t]
                            act.wait_ge(scores_filled, st.n + 1)
                            if st.n >= 4:
                                act.wait_ge(values_done, st.n // 2 - 1)
                            nc.scalar.activation(probs[0:nk, st.n % 4, :], score_bank[st.n % 2][0:nk, :], ACT.Exp,
                                                 scale=a.scale).then_inc(probs_ready, 1)
                        elif st.kind == "norm":
                            if st.n >= 1:
                                act.wait_ge(heads_ready, st.n)
                            act.wait_ge(values_done, at["values", st.G.n] + 1)
                            if not a.wide:
                                nc.scalar.activation(unnormed[:], value_bank[:], ACT.Identity)\
                                    .then_inc(unnormed_ready, 1)
                                act.wait_ge(denom_filled, st.narrow + 1)
                            link(nc.scalar.activation(recip[:], denom_bank[:], ACT.Ln))
                            nc.scalar.activation(recip[:], recip[:], ACT.Exp, scale=-1.0).then_inc(recip_ready, 1)
                        elif st.kind == "up":
                            func = {0: ACT.Gelu, 1: ACT.Silu, 2: ACT.Gelu, 3: ACT.Gelu_apprx_tanh}[st.layer]
                            bias = {0: f"L0ff_b1_{st.c}", 2: f"L2ff_g_{st.c}", 3: f"L3ff_b1_{st.c}"}
                            act.wait_ge(bank_filled, i + 1)
                            nc.scalar.activation(hidden[:, st.c, :], bank_at(i)[:], func,
                                                 bias=v_col(bias[st.layer]) if st.layer in bias else 0.0)\
                                .then_inc(bank_done[i % 2], 1)
                            if st.c == FC - 1:
                                load_exp_ln()

                @block.vector
                def _(dve):
                    chain = [0]

                    def link(ins):
                        chain[0] += 1
                        ins.then_inc(vector_chain, 1)
                        dve.wait_ge(vector_chain, chain[0])

                    nc.vector.tensor_copy(cur[:], mods[:, :, bass.ds(pair * SLOTS, SLOTS)]).then_inc(slots_ready, 1)
                    nc.vector.tensor_copy(ctx_cur[:], ctx_all[:, :, bass.ds(pair * (SLOTS * NC), SLOTS * NC)])\
                        .then_inc(slots_ready, 1)
                    dve.wait_ge(rest_loaded, 16)
                    for st in plan:
                        a = st.a
                        i = st.bank
                        if st.kind == "mean":
                            dve.wait_ge(bank_filled, i + 1)
                            if st.n >= 1:
                                dve.wait_ge(h_ready, st.n)
                            src = hs[:, st.s, :] if st.head_norm else xs[:, st.s, :]
                            nc.vector.tensor_tensor(centred[:], src, bank_at(i)[:], ALU.subtract)\
                                .then_inc(bank_done[i % 2], 1)
                        elif st.kind == "var":
                            dve.wait_ge(rstd_ready, st.n + 1)
                            nc.vector.tensor_tensor(centred[:], centred[:], rstd[:], ALU.mult)\
                                .then_inc(normed_ready, 1)
                        elif st.kind == "v" and not a.wide:
                            dve.wait_ge(bank_filled, i + 1)
                            n = a.tiles[st.t]
                            bias = w(a.name + "_bv" if a.name in ("L1c", "L3s") else "bv_ones")
                            nc.vector.tensor_tensor(vs[0:n, st.s, st.t, 0:512], bank_at(i)[0:n, :], bias[0:n, :],
                                                    ALU.add).then_inc(bank_done[i % 2], 1)
                        elif st.kind == "project":
                            G, part = st.G, st.part
                            n = a.keys if part == "k" else N
                            wait_ring_free(dve, G)
                            hi, lo = his[:, st.n % 2, 0:n], los[:, st.n % 2, 0:n]
                            if a.rope:
                                if st.n >= 1:
                                    dve.wait_ge(split_done, st.n)
                                    dve.wait_ge(hi_ready, st.n)
                                    dve.wait_ge(rope_sum, st.rope)
                                for k, (product, table) in enumerate(((rope_a, "rope_c"), (rope_b, "rope_s"))):
                                    dve.wait_ge(bank_filled, i + k + 1)
                                    nc.vector.tensor_tensor(product[:, 0:n], bank_at(i + k)[:, 0:n], w(table)[:, 0:n],
                                                            ALU.mult).then_inc(bank_done[(i + k) % 2], 1)
                                dve.wait_ge(hi_ready, st.n + 1)
                                link(nc.vector.tensor_tensor(lo, rope_a[:, 0:n], hi, ALU.subtract))
                            elif a.wide:
                                dve.wait_ge(hi_ready, st.n + 1)
                                nc.vector.tensor_tensor(lo, bank_at(i)[:, 0:n], hi, ALU.subtract)\
                                    .then_inc(bank_done[i % 2], 1)
                                wait_bank_done(dve, i)
                            else:
                                dve.wait_ge(hi_ready, st.n + 1)
                                if has_bias(a):
                                    bias = v_col(f"{a.name}_b{part}_{G.g}")
                                else:
                                    bias = v_col("kones") if part == "k" else 0.0
                                to = G.q_tile(ring, 0, 0) if part == "q" else lo
                                nc.vector.scalar_tensor_tensor(to, bank_at(i)[:, 0:n], bias, hi, ALU.add,
                                                               ALU.subtract).then_inc(bank_done[i % 2], 1)
                                wait_bank_done(dve, i)
                            if a.wide:
                                for j in range(2):
                                    rows = slice(64 * j, 64 * j + 64)
                                    if part == "q":
                                        nc.vector.tensor_copy(G.q_tile(ring, j, 0)[0:64, :], hi[rows, :])
                                        nc.vector.tensor_copy(G.q_tile(ring, j, 0)[64:128, :], hi[rows, :])
                                        last = nc.vector.tensor_copy(G.q_tile(ring, j, 1)[0:64, :], lo[rows, :])
                                    else:
                                        k1, k2 = G.k_tile(ring, small, j, 0), G.k_tile(ring, small, j, 1)
                                        nc.vector.tensor_copy(k1[0:64, 0:n], hi[rows, :])
                                        nc.vector.tensor_copy(k2[0:64, 0:n], hi[rows, :])
                                        last = nc.vector.tensor_copy(k1[64:128, 0:n], lo[rows, :])
                                last.then_inc(split_done, 1)
                            elif part == "k":
                                if st.sets:
                                    dve.wait_ge(operands_set, st.prepared)
                                for j in range(4):
                                    rows = slice(32 * j, 32 * j + 32)
                                    last = nc.vector.tensor_copy(G.k_tile(ring, small, j, 0)[rows, 0:n], lo[rows, :])
                                last.then_inc(split_done, 1)
                            else:
                                dve.sem_inc(split_done, 1)
                        elif st.kind == "max":
                            nk = a.keys
                            dve.wait_ge(max_filled, st.n + 1)
                            m = at["shift", st.G.n, st.j] % 8
                            if a.cross:
                                src = max_bank[st.n % 2][:, 0:QT * nk].rearrange("p (q k) -> p q k", k=nk)
                                to = neg_max[:, m, :]
                            else:
                                src, to = max_bank[st.n % 2][:], neg_max[:, m, st.t:st.t + 1]
                            nc.vector.tensor_reduce(to, src, AXIS_X, ALU.max, negate=True).then_inc(max_reduced, 1)
                        elif st.kind == "shift":
                            m = st.n % 8
                            dve.wait_ge(max_reduced, at["max", st.G.n, st.j] + 1)
                            if st.n >= 8:
                                dve.wait_ge(bank_filled, at["rows", at["shift_n", st.n - 8].n] + 1)
                            link(nc.vector.tensor_copy(shift_parts[:, m, :, 0], neg_max[:, m, :]))
                            nc.vector.tensor_tensor(shift_parts[:, m, :, 1], neg_max[:, m, :],
                                                    shift_parts[:, m, :, 0], ALU.subtract).then_inc(shift_split, 1)
                        elif st.kind == "rows" and not a.wide:
                            dve.wait_ge(bank_filled, i + 1)
                            q = st.G.q_tile(ring, 0, 0)
                            nc.vector.tensor_tensor(q, bank_at(i)[:], q, ALU.add).then_inc(bank_done[i % 2], 1)
                        elif st.kind == "norm":
                            dve.wait_ge(recip_ready, st.n + 1)
                            if st.n >= 2:
                                old = at["norm_n", st.n - 2]
                                dve.wait_ge(bank_filled, at["out", old.G.n] + 1)
                            nc.vector.tensor_tensor(heads_out[:, st.n % 2, :],
                                                    value_bank[:] if a.wide else unnormed[:], recip[:],
                                                    ALU.mult).then_inc(heads_ready, 1)
                        elif st.kind in ("out", "down"):
                            dve.wait_ge(bank_filled, i + 1)
                            wait_x(dve, st)
                            x = xs[:, st.s, :]
                            if st.kind == "out":
                                first = st.G.g == 0
                                gate = {"L1s": "L1ga_sa", "L1c": "L1ga_ca"}.get(a.name)
                                bias = f"L{a.layer}bo_{'ca' if a.cross else 'sa'}"
                            else:
                                first, gate, bias = True, "L1ga_ff" if st.layer == 1 else None, f"L{st.layer}ff_b2"
                            if gate is not None:
                                if first and st.kind == "out" and a.cross:
                                    link(nc.vector.tensor_scalar(x, x, mod("L1gb_ca", st.s), None, ALU.add))
                                nc.vector.scalar_tensor_tensor(x, bank_at(i)[:], mod(gate, st.s), x, ALU.mult,
                                                               ALU.add).then_inc(bank_done[i % 2], 1)
                            elif first:
                                nc.vector.scalar_tensor_tensor(x, bank_at(i)[:], v_col(bias), x, ALU.add,
                                                               ALU.add).then_inc(bank_done[i % 2], 1)
                            else:
                                nc.vector.tensor_tensor(x, bank_at(i)[:], x, ALU.add).then_inc(bank_done[i % 2], 1)
                        elif st.kind == "up" and st.layer in (1, 2):
                            wait_bank_done(dve, i)
                            i += 1
                            dve.wait_ge(bank_filled, i + 1)
                            hid = hidden[:, st.c, :]
                            nc.vector.scalar_tensor_tensor(
                                hid, bank_at(i)[:], v_col(f"L2ff_a_{st.c}") if st.layer == 2 else 0.0, hid,
                                ALU.add, ALU.mult).then_inc(bank_done[i % 2], 1)

                @block.gpsimd
                def _(pool):
                    chain = [0]

                    def link(ins):
                        chain[0] += 1
                        ins.then_inc(pool_chain, 1)
                        pool.wait_ge(pool_chain, chain[0])

                    for st in plan:
                        a, i = st.a, st.bank
                        if st.kind != "project":
                            continue
                        G = st.G
                        if st.clears or st.sets:
                            wait_ring_free(pool, G)
                        if st.clears:
                            for j in range(2):
                                last = nc.gpsimd.memset(G.q_tile(ring, j, 1)[64:128, :], 0.0)
                            last.then_inc(operands_set, 1)
                        elif st.sets and a.wide:
                            for j in range(2):
                                k2 = G.k_tile(ring, small, j, 1)
                                link(nc.gpsimd.memset(k2[64:128, :], 0.0))
                                last = nc.gpsimd.memset(k2[64 + 32 * j:66 + 32 * j, :], 1.0)
                                if j == 0:
                                    link(last)
                            last.then_inc(operands_set, 1)
                        elif st.sets:
                            if a.cross:
                                last = nc.gpsimd.memset(ring[:, G.region, 4 * G.half + 1, 0:4 * NC], 0.0)
                            else:
                                last = nc.gpsimd.memset(ring[:, G.region, 1:5, :], 0.0)
                            last.then_inc(operands_set, 1)
                        if st.clears or st.sets:
                            pool.wait_ge(operands_set, st.prepared)
                        if a.rope:
                            n = N if st.part == "q" else a.keys
                            wait_bank_done(pool, i)
                            wait_bank_done(pool, i + 1)
                            nc.gpsimd.tensor_tensor(rope_a[:, 0:n], rope_a[:, 0:n], rope_b[:, 0:n], ALU.add)\
                                .then_inc(rope_sum, 1)
                            pool.wait_ge(rope_sum, st.rope + 1)

            with nc.Block() as block:
                @block.gpsimd
                def _(pool):
                    for s in sems.values():
                        pool.sem_clear(s)


def rows128(m):
    return np.concatenate([m, np.zeros((P - m.shape[0], m.shape[1]), m.dtype)]) if m.shape[0] < P else m


def chunks(m):
    return m.reshape(-1, P, m.shape[1]).transpose(1, 0, 2).reshape(P, -1)


def head_blocks(m, copies):
    out = np.zeros((m.shape[0], H, 32), m.dtype)
    for c in copies:
        out[:, :, c:c + 8] = m.reshape(-1, H, 8)
    return out.reshape(m.shape[0], H * 32)


STACK = (8, 16, 24)
LOW_OF_Q, LOW_OF_K = 24, 16


def swap_pairs(m):
    return m.reshape(m.shape[0], -1, 2)[:, :, ::-1].reshape(m.shape)


def out_rows(m):
    out = np.zeros((4, 4, 32, P), m.dtype)
    out[:, :, 0:8, :] = m.reshape(4, 4, 8, P)
    return out.reshape(4, P, P).transpose(1, 0, 2).reshape(P, 4 * P)


def bias_groups(b, copies, ones=False):
    m = head_blocks(b.reshape(1, P), copies).reshape(4, P)
    if ones:
        m = m.copy()
        m.reshape(4, 4, 32)[:, :, 0:2] = 1.0
    return m


def kernel(**inputs):
    import concourse.bacc as bacc
    from concourse.bass_utils import run_bass_kernel_spmd

    I = {n: np.asarray(v) for n, v in inputs.items()}
    f32 = np.float32
    L0 = {n[9:]: v for n, v in I.items() if n.startswith("L0_xcond_")}
    L1 = {n[9:]: v for n, v in I.items() if n.startswith("L1_xcond_")}
    L2 = {n[9:]: v for n, v in I.items() if n.startswith("L2_xcond_")}
    L3 = {n[9:]: v for n, v in I.items() if n.startswith("L3_xcond_")}

    ada1 = L1["adaln_w"].T
    order1 = ["L1sh_sa", "L1sc_sa", "L1ga_sa", "L1sh_ca", "L1sc_ca", "L1ga_ca", "L1sh_ff", "L1sc_ff", "L1ga_ff"]
    order3 = ["L3sh_msa", "L3sc_msa", "L3sh_x", "L3sc_x", "L3sh_mlp", "L3sc_mlp"]
    mw = {"L0g1": (L0["g1_w"], L0["g1_b"]), "L0b1": (L0["b1_w"], L0["b1_b"]),
          "L0g2": (L0["g2_w"], L0["g2_b"]), "L0b2": (L0["b2_w"], L0["b2_b"])}
    for i, n in enumerate(order1):
        mw[n] = (ada1[:, i * P:(i + 1) * P], L1["adaln_b"][i * P:(i + 1) * P])
    for i in range(3):
        for j, n in enumerate((f"L2s{i + 1}", f"L2t{i + 1}")):
            mw[n] = (L2[f"n{i + 1}_w"][:, j * P:(j + 1) * P], L2[f"n{i + 1}_b"][j * P:(j + 1) * P])
    for i, n in enumerate(order3):
        mw[n] = (L3["W_ada"][:, i * P:(i + 1) * P], L3["b_ada"][i * P:(i + 1) * P])
    mod_w = np.concatenate([mw[n][0] for n in MOD_SCALES + MOD_REST], 1)
    mod_b = np.stack([mw[n][1] for n in MOD_SCALES + MOD_REST], 1)

    vec = {"eps5": np.full(P, 1e-5, f32), "eps6": np.full(P, 1e-6, f32),
           "lw1": L0["ln1_w"], "lb1": L0["ln1_b"], "lw2": L0["ln2_w"], "lb2": L0["ln2_b"],
           "cw": rows128(L0["ca_lnc_w"][:, None])[:, 0], "cb": rows128(L0["ca_lnc_b"][:, None])[:, 0],
           "L1cond_b": L1["cond_b"], "L3b_ctx": L3["b_ctx"], "L1bo_ca": L1["ca_out_b"],
           "L0bo_sa": L0["sa_bo"], "L0bo_ca": L0["ca_bo"], "L0ff_b2": L0["ff_b2"],
           "L2bo_sa": L2["o1_b"], "L2bo_ca": L2["o2_b"], "L2ff_b2": L2["ff_b2"],
           "L3bo_sa": L3["b_proj"], "L3bo_ca": L3["b_out"], "L3ff_b2": L3["b_fc2"]}
    for n in ("qn_w", "qn_b", "kn_w", "kn_b"):
        vec[n] = np.tile(L1[n], H)
    block = np.arange(P) % 32
    vec["qmask"] = (block >= LOW_OF_Q).astype(f32)
    vec["kmask"] = ((block >= LOW_OF_K) & (block < LOW_OF_K + 8)).astype(f32)
    vec["kones"] = (block < 2).astype(f32)
    for c in range(FC):
        sl = slice(c * P, (c + 1) * P)
        vec[f"L0ff_b1_{c}"], vec[f"L3ff_b1_{c}"] = L0["ff_b1"][sl], L3["b_fc1"][sl]
        vec[f"L2ff_a_{c}"], vec[f"L2ff_g_{c}"] = L2["ff_b1"][0:FF][sl], L2["ff_b1"][FF:][sl]
    for name, bias in (("L1c", L1["ca_in_b"]), ("L3s", L3["b_qkv"])):
        for i, part in enumerate("qk"):
            b = bias[i * P:(i + 1) * P]
            full = bias_groups(b, STACK, ones=part == "k")
            low = bias_groups(b, (LOW_OF_Q if part == "q" else LOW_OF_K,))
            for g in range(4):
                vec[f"{name}_b{part}_{g}"], vec[f"{name}_b{part}m_{g}"] = full[g], low[g]
    vec = np.stack([vec[n] for n in VECS], 1)

    def v_bias(b):
        m = head_blocks(b.reshape(1, P), (0,)).copy()
        m.reshape(H, 32)[:, 8] = 1.0
        return np.repeat(m, P, 0)

    eye = np.eye(P, dtype=f32)
    avg8 = np.kron(np.eye(H, dtype=f32), np.full((8, 8), 0.125, f32))
    dsel = np.zeros((P, P), f32)
    for j in range(4):
        dsel[32 * j + 8, 32 * j:32 * j + 32] = 1.0
    inv = (f32(1.0) / f32(10000.0) ** (np.arange(0, 64, 2, dtype=f32) / f32(64))).astype(f32)
    ang = (np.arange(N, dtype=f32)[:, None] * inv[None, :]).astype(f32)
    rope_c = np.tile(np.repeat(np.cos(ang).T, 2, 0), (2, 1)).astype(f32)
    sign = np.tile(np.array([-1.0, 1.0], f32), P // 2)[:, None]
    rope_s = (np.tile(np.repeat(np.sin(ang).T, 2, 0), (2, 1)) * sign).astype(f32)
    ca_in, qkv3 = L1["ca_in_w"].T, L3["W_qkv"]
    part3 = [qkv3[:, i * P:(i + 1) * P] for i in range(3)]
    kept = {
        "avg": np.full((P, P), 1.0 / P, f32), "avg8": avg8, "dsel": dsel, "ones": np.ones((P, 64), f32),
        "rope_c": rope_c, "rope_s": rope_s,
        "L0ff1": L0["ff_w1"], "L0ff2": chunks(L0["ff_w2"]),
        "pick_qk": head_blocks(eye, STACK), "pick_v": head_blocks(eye, (0,)), "L1s_wo": out_rows(eye),
        "L1c_q": head_blocks(ca_in[:, 0:P], STACK), "L1c_k": head_blocks(ca_in[:, P:2 * P], STACK),
        "L1c_v": head_blocks(ca_in[:, 2 * P:], (0,)), "L1c_wo": out_rows(L1["ca_out_w"].T),
        "L1w1": L1["w1"].T, "L1w3": L1["w3"].T, "L1w2": chunks(L1["w2"].T), "L1c_bv": v_bias(L1["ca_in_b"][2 * P:]),
        "L2ff1": L2["ff_w1"], "L2ff2": chunks(L2["ff_w2"]),
        "L3s_q": head_blocks(part3[0], STACK), "L3s_k": head_blocks(part3[1], STACK),
        "L3s_v": head_blocks(part3[2], (0,)), "L3s_wo": out_rows(L3["W_proj"]), "L3s_bv": v_bias(L3["b_qkv"][2 * P:]),
        "L3c_q": head_blocks(L3["W_q"], STACK), "L3c_k": head_blocks(L3["W_k"], STACK),
        "L3c_v": head_blocks(L3["W_v"], (0,)), "L3c_wo": out_rows(L3["W_out"]),
        "L3ff1": L3["W_fc1"], "L3ff2": chunks(L3["W_fc2"]),
        "bv_ones": v_bias(np.zeros(P, f32)),
    }
    kept = np.concatenate([kept[n] for n, _ in KEPT], 1)

    def wide_weights(q, k, v, o, swapped):
        parts = [rows128(q), rows128(k), rows128(v), chunks(o)]
        if swapped:
            parts += [rows128(swap_pairs(q)), rows128(swap_pairs(k))]
        return np.concatenate(parts, 1)

    mid = H * 64
    arrays = {
        "x_in": I["x"].reshape(B * N, D).T, "ctx_in": I["ctx_768"].reshape(B * NC, DC).T,
        "cond_in": I["cond_1024"].T, "vec_in": vec, "ident_in": np.eye(P).astype(mybir.dt.np(BF16)),
        "mod_w_in": mod_w, "mod_b_in": mod_b,
        "cond_w_in": np.concatenate([rows128(L1["cond_w"].T), rows128(L3["W_ctx"])], 1),
        "kept_in": kept,
        "self0_in": wide_weights(L0["sa_wq"], L0["sa_wkv"][:, 0:mid], L0["sa_wkv"][:, mid:], L0["sa_wo"], True),
        "cross0_in": wide_weights(L0["ca_wq"], L0["ca_wkv"][:, 0:mid], L0["ca_wkv"][:, mid:], L0["ca_wo"], True),
        "self2_in": wide_weights(L2["q1"], L2["k1"], L2["v1"], L2["o1_w"], False),
        "cross2_in": wide_weights(L2["q2"], L2["k2"], L2["v2"], L2["o2_w"], False),
    }
    arrays = {n: np.ascontiguousarray(a) for n, a in arrays.items()}
    nc = bacc.Bacc("TRN2", target_bir_lowering=False, num_devices=1, dynamic_dma_scratch_size=1024)
    args = [nc.dram_tensor(n, a.shape, mybir.dt.from_np(a.dtype), kind="ExternalInput").ap()
            for n, a in arrays.items()]
    out = nc.dram_tensor("out", (P, B * N), F32, kind="ExternalOutput").ap()
    build(nc, *args, out)
    r = run_bass_kernel_spmd(nc, [arrays], core_ids=[0])
    return r.results[0]["out"].T.reshape(B, N, D)
```
